# Optimizing a Trainium2 kernel written in Bass

```python
import numpy as np
import jax
import jax.numpy as jnp

def _softmax(x, axis=-1):
    return jax.nn.softmax(x, axis=axis)

def _gelu(x):
    return jax.nn.gelu(x, approximate=True)

def _silu(x):
    return jax.nn.silu(x)

def _sigmoid(x):
    return jax.nn.sigmoid(x)

def _layernorm(x, axis=-1, eps=1e-05):
    m = jnp.mean(x, axis=axis, keepdims=True)
    v = jnp.var(x, axis=axis, keepdims=True)
    return (x - m) / jnp.sqrt(v + eps)

def _scatter_add(tgt, idx, src, axis=0):
    return tgt.at[idx].add(src)

def _segment_sum(src, seg, n):
    return jax.ops.segment_sum(src, seg, n)
kernel_name = 'mk_adaln_d1_jaxref_r8_52db2d'

def setup_inputs(seed: int=0):
    np.random.seed(seed)
    _w = jnp.asarray

    def _L0_attn_setup():
        import jax, jax.numpy as jnp
        import numpy as np
        B, S, HID, NH = (4, 512, 128, 16)
        D = HID // NH
        EPS = 1e-05

        def _delta_scan(q, k, v, beta):
            vsum = v.sum(-1)
            qs = jnp.moveaxis(q, 1, 0)
            ks_ = jnp.moveaxis(k, 1, 0)
            vs = jnp.moveaxis(vsum, 1, 0)
            bs = jnp.moveaxis(beta, 1, 0)

            def step(h, inp):
                q_t, k_t, vsum_t, beta_t = inp
                h = h * beta_t[..., None, None]
                h = h + (k_t * vsum_t[..., None])[:, :, None, :]
                o_t = jnp.einsum('bhj,bhjk->bhk', q_t, h)
                return (h, o_t)
            h0 = jnp.zeros((q.shape[0], q.shape[2], D, D), dtype=q.dtype)
            _, o = jax.lax.scan(step, h0, (qs, ks_, vs, bs))
            return jnp.moveaxis(o, 0, 1)
        key = jax.random.key(seed)
        ks = jax.random.split(key, 8)
        x = jax.random.normal(ks[0], (B, S, HID), dtype=jnp.float32)
        sc = 0.03
        Wq = jax.random.normal(ks[1], (HID, HID), dtype=jnp.float32) * sc
        Wk = jax.random.normal(ks[2], (HID, HID), dtype=jnp.float32) * sc
        Wv = jax.random.normal(ks[3], (HID, HID), dtype=jnp.float32) * sc
        Wbeta = jax.random.normal(ks[4], (HID, NH), dtype=jnp.float32) * sc
        b_beta = jnp.full((NH,), 0.9, dtype=jnp.float32)
        Wo = jax.random.normal(ks[5], (HID, HID), dtype=jnp.float32) * sc
        b_o = jnp.zeros((HID,), dtype=jnp.float32)
        ln_g = jnp.ones((HID,), dtype=jnp.float32)
        ln_b = jnp.zeros((HID,), dtype=jnp.float32)
        return {'x': x, 'Wq': Wq, 'Wk': Wk, 'Wv': Wv, 'Wbeta': Wbeta, 'b_beta': b_beta, 'Wo': Wo, 'b_o': b_o, 'ln_g': ln_g, 'ln_b': ln_b}
    _L0_attn_in = _L0_attn_setup()

    def _L0_ffn_setup():
        import jax, jax.numpy as jnp
        import numpy as np
        E = 8
        K = 2
        C = 128
        F = 256
        EPS = 1e-05
        key = jax.random.key(seed)
        ks = jax.random.split(key, 6)
        x = jax.random.normal(ks[0], (2, 128, C), dtype=jnp.float32)
        ln_gamma = 1.0 + 0.02 * jax.random.normal(ks[1], (C,), dtype=jnp.float32)
        ln_beta = 0.02 * jax.random.normal(ks[2], (C,), dtype=jnp.float32)
        gate_w = jax.random.normal(ks[3], (E, C), dtype=jnp.float32) / np.sqrt(C)
        w1 = jax.random.normal(ks[4], (E, F, C), dtype=jnp.float32) / np.sqrt(C)
        w2 = jax.random.normal(ks[5], (E, C, F), dtype=jnp.float32) / np.sqrt(F)
        return {'x': x, 'ln_gamma': ln_gamma, 'ln_beta': ln_beta, 'gate_w': gate_w, 'w1': w1, 'w2': w2}
    _L0_ffn_in = _L0_ffn_setup()
    _L0_c = _w((lambda *s: np.random.randn(*s).astype(np.float32) * 0.05)(8, 128))
    _L0_wmod = _w((lambda *s: np.random.randn(*s).astype(np.float32) * 0.05)(128, 6 * 128) * 128 ** (-0.5))
    _d = {'L0_attn_x': _L0_attn_in['x'], 'L0_attn_Wq': _L0_attn_in['Wq'], 'L0_attn_Wk': _L0_attn_in['Wk'], 'L0_attn_Wv': _L0_attn_in['Wv'], 'L0_attn_Wbeta': _L0_attn_in['Wbeta'], 'L0_attn_b_beta': _L0_attn_in['b_beta'], 'L0_attn_Wo': _L0_attn_in['Wo'], 'L0_attn_b_o': _L0_attn_in['b_o'], 'L0_attn_ln_g': _L0_attn_in['ln_g'], 'L0_attn_ln_b': _L0_attn_in['ln_b'], 'L0_ffn_ln_gamma': _L0_ffn_in['ln_gamma'], 'L0_ffn_ln_beta': _L0_ffn_in['ln_beta'], 'L0_ffn_gate_w': _L0_ffn_in['gate_w'], 'L0_ffn_w1': _L0_ffn_in['w1'], 'L0_ffn_w2': _L0_ffn_in['w2'], 'L0_c': _L0_c, 'L0_wmod': _L0_wmod}
    _x0 = _d['L0_attn_x']
    _d['L0_attn_x'] = jax.random.normal(jax.random.fold_in(jax.random.key(seed), 1), (8, 1024, 128), dtype=_x0.dtype)
    del _x0
    return _d

def reference(L0_attn_x, L0_attn_Wq, L0_attn_Wk, L0_attn_Wv, L0_attn_Wbeta, L0_attn_b_beta, L0_attn_Wo, L0_attn_b_o, L0_attn_ln_g, L0_attn_ln_b, L0_ffn_ln_gamma, L0_ffn_ln_beta, L0_ffn_gate_w, L0_ffn_w1, L0_ffn_w2, L0_c, L0_wmod):

    def _L0_attn_ref(x, Wq, Wk, Wv, Wbeta, b_beta, Wo, b_o, ln_g, ln_b):
        import jax, jax.numpy as jnp
        import numpy as np
        B, S, HID, NH = (4, 512, 128, 16)
        D = HID // NH
        EPS = 1e-05

        def _delta_scan(q, k, v, beta):
            vsum = v.sum(-1)
            qs = jnp.moveaxis(q, 1, 0)
            ks_ = jnp.moveaxis(k, 1, 0)
            vs = jnp.moveaxis(vsum, 1, 0)
            bs = jnp.moveaxis(beta, 1, 0)

            def step(h, inp):
                q_t, k_t, vsum_t, beta_t = inp
                h = h * beta_t[..., None, None]
                h = h + (k_t * vsum_t[..., None])[:, :, None, :]
                o_t = jnp.einsum('bhj,bhjk->bhk', q_t, h)
                return (h, o_t)
            h0 = jnp.zeros((q.shape[0], q.shape[2], D, D), dtype=q.dtype)
            _, o = jax.lax.scan(step, h0, (qs, ks_, vs, bs))
            return jnp.moveaxis(o, 0, 1)
        b, s, hid = x.shape
        residual = x
        q = (x @ Wq).reshape(b, s, NH, D)
        k = (x @ Wk).reshape(b, s, NH, D)
        v = (x @ Wv).reshape(b, s, NH, D)
        beta = jax.nn.sigmoid(x @ Wbeta + b_beta)
        o = _delta_scan(q, k, v, beta).reshape(b, s, hid)
        out = o @ Wo + b_o
        y = residual + out
        mu = y.mean(-1, keepdims=True)
        var = ((y - mu) ** 2).mean(-1, keepdims=True)
        return ln_g * (y - mu) * jax.lax.rsqrt(var + EPS) + ln_b

    def _L0_ffn_ref(x, ln_gamma, ln_beta, gate_w, w1, w2):
        import jax, jax.numpy as jnp
        import numpy as np
        E = 8
        K = 2
        C = 128
        F = 256
        EPS = 1e-05
        B, T, Cc = x.shape
        xf = x.reshape(-1, Cc)
        mu = jnp.mean(xf, axis=-1, keepdims=True)
        var = jnp.var(xf, axis=-1, keepdims=True)
        rn = (xf - mu) * jax.lax.rsqrt(var + EPS) * ln_gamma + ln_beta
        logits = rn @ gate_w.T
        probs = jax.nn.softmax(logits, axis=-1)
        rw, sel = jax.lax.top_k(probs, K)
        comb = jnp.sum(jax.nn.one_hot(sel, E, dtype=xf.dtype) * rw[..., None], axis=1)
        h = jax.nn.gelu(jnp.einsum('nc,efc->enf', xf, w1), approximate=False)
        y = jnp.einsum('enf,ecf->enc', h, w2)
        out = jnp.einsum('enc,ne->nc', y, comb)
        return out.reshape(B, T, Cc)
    x = L0_attn_x
    mod = (_silu(L0_c) @ L0_wmod).reshape(L0_c.shape[0], 6, 1, -1)
    sa, ca, ga, sb, cb, gb = (mod[:, 0], mod[:, 1], mod[:, 2], mod[:, 3], mod[:, 4], mod[:, 5])
    ga = (2 * (ga >= 0) - 1) * jnp.maximum(jnp.abs(ga), 0.25)
    gb = (2 * (gb >= 0) - 1) * jnp.maximum(jnp.abs(gb), 0.25)
    h = _layernorm(x, axis=-1) * (1 + ca) + sa
    x = x + ga * _L0_attn_ref(h, L0_attn_Wq, L0_attn_Wk, L0_attn_Wv, L0_attn_Wbeta, L0_attn_b_beta, L0_attn_Wo, L0_attn_b_o, L0_attn_ln_g, L0_attn_ln_b)
    h = _layernorm(x, axis=-1) * (1 + cb) + sb
    x = x + gb * _L0_ffn_ref(h, L0_ffn_ln_gamma, L0_ffn_ln_beta, L0_ffn_gate_w, L0_ffn_w1, L0_ffn_w2)
    return x

_drawn_inputs = setup_inputs


def setup_inputs(seed=0):
    import zlib

    import numpy as np

    out = dict(_drawn_inputs(seed))
    spreads = {'L0_attn_b_beta': (0.8999999761581421, 0.6),
     'L0_attn_b_o': (0.0, 0.296),
     'L0_attn_ln_g': (1.0, 0.2),
     'L0_attn_ln_b': (0.0, 0.296)}
    factors = {'L0_attn_Wbeta': 24.495, 'L0_ffn_ln_gamma': 200.0, 'L0_ffn_ln_beta': 198.925}
    for name, (base, spread) in spreads.items():
        noise = np.random.default_rng([zlib.crc32(name.encode()), seed]).standard_normal(out[name].shape)
        drawn = base * np.exp(spread * noise) if base else spread * noise
        out[name] = jnp.asarray(drawn.astype(out[name].dtype))
    for name, factor in factors.items():
        out[name] = (out[name] * factor).astype(out[name].dtype)
    return out
```

```python
from contextlib import ExitStack

import concourse.bass as bass
from concourse import mybir

F32 = mybir.dt.float32
F32R = mybir.dt.float32r
U32 = mybir.dt.uint32
ALU = mybir.AluOpType
ACT = mybir.ActivationFunctionType
AX_X = mybir.AxisListType.X

P = 128
TILES = 4
TOK = TILES * P
EPS = 1e-5
GATE_FLOOR = 0.25
EXP_SQUARINGS = 4


class Group:

    def __init__(self, b, k):
        self.b, self.k = b, k

    def __add__(self, n):
        return Group(self.b, self.k + n)

    def __sub__(self, n):
        return Group(self.b, self.k - n)

    @property
    def slot(self):
        return self.k % 2

    @property
    def number(self):
        return 2 * self.b + self.k

    @property
    def batch(self):
        return self.b + self.k // 2


def exists(group):
    return not isinstance(group.b, int) or group.number >= 0


def nth(group, per, n):
    return (2 * per) * group.b + (per * group.k + n)


def turn(group, by=16):
    return by * group.b + by * (group.k // 2 + 1)


def adaln_moe_kernel(nc, x, cT, wmod, wq, wk, wv, wbeta, b_beta, wo, b_o, ln_g, ln_b, gamma, beta_, gateT,
                     w1T, w2T, out):
    GROUPS = x.shape[0]
    BATCHES = cT.shape[1]
    HEADS = wbeta.shape[1]
    D = P // HEADS
    E = gateT.shape[1]
    assert GROUPS == 2 * BATCHES and E == 8

    with ExitStack() as ctx:
        def sb(name, shape, dt=F32):
            return ctx.enter_context(nc.sbuf_tensor(name, shape, dt))

        def psum(name, shape):
            return ctx.enter_context(nc.psum_tensor(name, shape, F32))

        def sem(name):
            return ctx.enter_context(nc.semaphore(name))

        up_ps = psum("up_ps", [P, 2, 2, TOK])
        down_ps = psum("down_ps", [P, TOK])
        ps0 = psum("ps0", [P, TOK])
        ps1 = psum("ps1", [P, TOK])
        ps2 = psum("ps2", [P, TOK])

        ident = sb("ident", [P, P])
        minus_half = sb("minus_half", [P, TILES])
        expert_ids = sb("expert_ids", [P, TILES, E])
        w1 = sb("w1", [P, E * 256])
        w1_hi = sb("w1_hi", [P, E * 256], F32R)
        w1_lo = sb("w1_lo", [P, E * 256], F32R)
        w2 = sb("w2", [P, E, 2, P])
        attn_w = sb("attn_w", [P, 5, P])
        attn_hi = sb("attn_hi", [P, 5, P], F32R)
        attn_lo = sb("attn_lo", [P, 5, P], F32R)
        Q, K, V, BETA, OUT = range(5)
        wq_sb = sb("wq_sb", [P, P])
        wv_sb = sb("wv_sb", [P, P])
        wbeta_sb = sb("wbeta_sb", [P, HEADS])
        head_sums = sb("head_sums", [P, 2, HEADS])
        cols = sb("cols", [P, 4])
        half_b_beta = sb("half_b_beta", [P, 1])
        gate = sb("gate", [P, E])
        wmod_sb = sb("wmod_sb", [P, 6 * P])
        c_sb = sb("c_sb", [P, BATCHES])
        c_tanh = sb("c_tanh", [P, BATCHES])
        c_sig = sb("c_sig", [P, BATCHES])
        silu_c = sb("silu_c", [P, BATCHES])
        silu_rows = sb("silu_rows", [P, BATCHES, P])
        mod_cols = sb("mod_cols", [P, 3, BATCHES])
        gate_sign = sb("gate_sign", [P, P])
        gate_abs = sb("gate_abs", [P, P])
        lng_rows = sb("lng_rows", [P, P])
        lnb_rows = sb("lnb_rows", [P, P])
        ga_rows = sb("ga_rows", [P, P])
        scale_a = sb("scale_a", [P, BATCHES, P])
        shift_a = sb("shift_a", [P, BATCHES, P])
        scale_b = sb("scale_b", [P, BATCHES, P])
        shift_b = sb("shift_b", [P, BATCHES, P])

        x_tm = sb("x_tm", [P, 2, TOK])
        ln1_bn = sb("ln1_bn", [P, TILES, 6])
        ln1_mv = sb("ln1_mv", [P, TILES, 2])
        ln1_ve = sb("ln1_ve", [P, TILES])
        ln1_r = sb("ln1_r", [P, TILES])
        n1_tm = sb("n1_tm", [P, TOK])
        h_cm = sb("h_cm", [P, TOK])
        h_hi = sb("h_hi", [P, TOK], F32R)
        h_lo = sb("h_lo", [P, TOK], F32R)
        beta_tanh = sb("beta_tanh", [P, TOK])
        beta_cm = sb("beta_cm", [P, TOK])
        vsum_cm = sb("vsum_cm", [P, TOK])
        kv_cm = sb("kv_cm", [P, TOK])
        state_cm = sb("state_cm", [P, 2, TOK])
        o_cm = sb("o_cm", [P, TOK])
        o_hi = sb("o_hi", [P, TOK], F32R)
        o_lo = sb("o_lo", [P, TOK], F32R)
        z_cm = sb("z_cm", [P, TOK])
        xb_tm = sb("xb_tm", [P, 2, TOK])

        lnz_bn = sb("lnz_bn", [P, TILES, 6])
        lnz_mv = sb("lnz_mv", [P, TILES, 2])
        lnz_ve = sb("lnz_ve", [P, TILES])
        lnz_r = sb("lnz_r", [P, TILES])
        nz_tm = sb("nz_tm", [P, TOK])
        nza_tm = sb("nza_tm", [P, TOK])
        x2_tm = sb("x2_tm", [P, 4 * TOK])
        ln2_bn = sb("ln2_bn", [P, TILES, 6])
        ln2_mv = sb("ln2_mv", [P, TILES, 2])
        ln2_ve = sb("ln2_ve", [P, TILES])
        ln2_r = sb("ln2_r", [P, TILES])
        n2_tm = sb("n2_tm", [P, TOK])
        n2c_tm = sb("n2c_tm", [P, TOK])
        h2_tm = sb("h2_tm", [P, TOK])
        ln3_bn = sb("ln3_bn", [P, TILES, 6])
        ln3_mv = sb("ln3_mv", [P, TILES, 2])
        ln3_ve = sb("ln3_ve", [P, TILES])
        ln3_r = sb("ln3_r", [P, TILES])
        rn_tm = sb("rn_tm", [P, TOK])
        rn_cm = sb("rn_cm", [P, TOK])
        logits = sb("logits", [P, TILES, E])
        top = sb("top", [P, TILES, 8])
        top_ids = sb("top_ids", [P, TILES, 8], U32)
        below = sb("below", [P, TILES, E])
        exp_tanh = sb("exp_tanh", [P, TILES, E])
        exp_den = sb("exp_den", [P, TILES, E])
        exp_rec = sb("exp_rec", [P, TILES, E])
        powers = sb("powers", [P, EXP_SQUARINGS + 1, TILES, E])
        is_first = sb("is_first", [P, TILES, E])
        is_second = sb("is_second", [P, TILES, E])
        chosen = sb("chosen", [P, TILES, E])
        exp_sum = sb("exp_sum", [P, TILES])
        exp_sum_rec = sb("exp_sum_rec", [P, TILES])
        exp_chosen = sb("exp_chosen", [P, TILES, E])
        comb_tm = sb("comb_tm", [P, E, TILES])
        comb_em = sb("comb_em", [E * TILES, P])
        comb_row = sb("comb_row", [1, E * TOK])
        h2_hi = sb("h2_hi", [P, 2, TOK], F32R)
        h2_lo = sb("h2_lo", [P, 2, TOK], F32R)

        comb_cm = sb("comb_cm", [P, 4, TOK])
        gelu_cm = sb("gelu_cm", [P, 2, 2, TOK])
        scaled_cm = sb("scaled_cm", [P, 2, TOK])
        sum_cm = sb("sum_cm", [P, 2, TOK])
        gated_cm = sb("gated_cm", [P, TOK])
        out_tm = sb("out_tm", [P, 2, TOK])

        s_weights = {n: sem("loaded_" + n) for n in
                     ("c", "wmod", "wq", "wk", "wv", "wbeta", "wo", "cols", "rows", "gate", "w1", "w2")}
        x_loaded = [sem("x_loaded0"), sem("x_loaded1")]
        row_loaded = sem("row_loaded")
        stored = [sem("stored0"), sem("stored1")]
        ident_zero = sem("ident_zero")
        consts = sem("consts")
        setup_v = sem("setup_v")
        setup_a = sem("setup_a")
        setup_p = sem("setup_p")
        ln1_bn_done = sem("ln1_bn_done")
        ln1_mv_done = sem("ln1_mv_done")
        ln1_ve_done = sem("ln1_ve_done")
        ln1_r_done = sem("ln1_r_done")
        n1_done = sem("n1_done")
        n1_turned = sem("n1_turned")
        h_done = sem("h_done")
        h_hi_done = sem("h_hi_done")
        h_lo_done = sem("h_lo_done")
        beta_ps_done = sem("beta_ps_done")
        v_ps_done = sem("v_ps_done")
        k_ps_done = sem("k_ps_done")
        q_ps_done = sem("q_ps_done")
        beta_tanh_done = sem("beta_tanh_done")
        vsum_done = sem("vsum_done")
        beta_done = sem("beta_done")
        kv_done = sem("kv_done")
        scan_done = sem("scan_done")
        o_done = sem("o_done")
        o_hi_done = sem("o_hi_done")
        o_lo_done = sem("o_lo_done")
        out_ps_done = sem("out_ps_done")
        z_done = sem("z_done")
        xb_done = sem("xb_done")
        z_turned = sem("z_turned")
        lnz_bn_done = sem("lnz_bn_done")
        lnz_mv_done = sem("lnz_mv_done")
        lnz_ve_done = sem("lnz_ve_done")
        lnz_r_done = sem("lnz_r_done")
        nz_done = sem("nz_done")
        nza_done = sem("nza_done")
        x2_done = sem("x2_done")
        ln2_bn_done = sem("ln2_bn_done")
        ln2_mv_done = sem("ln2_mv_done")
        ln2_ve_done = sem("ln2_ve_done")
        ln2_r_done = sem("ln2_r_done")
        n2_done = sem("n2_done")
        n2c_done = sem("n2c_done")
        h2_done = sem("h2_done")
        ln3_bn_done = sem("ln3_bn_done")
        ln3_mv_done = sem("ln3_mv_done")
        ln3_ve_done = sem("ln3_ve_done")
        ln3_r_done = sem("ln3_r_done")
        rn_done = sem("rn_done")
        rn_turned = sem("rn_turned")
        rn_cm_done = sem("rn_cm_done")
        logits_ps_done = sem("logits_ps_done")
        logits_done = sem("logits_done")
        top_done = sem("top_done")
        below_done = sem("below_done")
        exp_tanh_done = sem("exp_tanh_done")
        top_ids_done = sem("top_ids_done")
        den_done = sem("den_done")
        is_top_done = sem("is_top_done")
        rec_done = sem("rec_done")
        chosen_done = sem("chosen_done")
        root_done = sem("root_done")
        squared = sem("squared")
        exp_chosen_done = sem("exp_chosen_done")
        exp_sum_done = sem("exp_sum_done")
        exp_sum_rec_done = sem("exp_sum_rec_done")
        comb_done = sem("comb_done")
        comb_turned = sem("comb_turned")
        comb_em_done = sem("comb_em_done")
        comb_spread = sem("comb_spread")
        h2_turned = sem("h2_turned")
        h2_hi_done = sem("h2_hi_done")
        h2_lo_done = sem("h2_lo_done")
        up_done = sem("up_done")
        gelu_done = sem("gelu_done")
        down_done = sem("down_done")
        scaled_done = sem("scaled_done")
        sum_done = sem("sum_done")
        gated_done = sem("gated_done")
        gated_turned = sem("gated_turned")
        out_done = sem("out_done")

        block = ctx.enter_context(nc.Block())

        def run(engine, slot):
            def step(experts, late, early):
                for s in range(E):
                    slot(s, experts, late, early)

            step(None, None, Group(0, 0))
            step(None, Group(0, 0), Group(0, 1))
            for k in range(2):
                step(Group(0, k), Group(0, k + 1), Group(0, k + 2))
            with engine.Fori(1, BATCHES - 2) as b:
                for k in range(2):
                    step(Group(b, k), Group(b, k + 1), Group(b, k + 2))
            for k in range(2):
                step(Group(BATCHES - 2, k), Group(BATCHES - 2, k + 1), Group(BATCHES - 2, k + 2))
            last = BATCHES - 1
            step(Group(last, 0), Group(last, 1), None)
            step(Group(last, 1), None, None)

        def tile(t):
            return slice(t * P, (t + 1) * P)

        def tiles_of(rows):
            return lambda t: rows[:, tile(t)]

        SETUP_V_SILU = 3
        SETUP_V_COLS = 6
        SETUP_V_HALF = 7
        SETUP_V_BETA = 10
        SETUP_V_V = 14
        SETUP_V_K = 16
        SETUP_V_Q = 20
        SETUP_V_OUT = 22
        SETUP_V_SHIFT = 22 + 8 * BATCHES
        SETUP_V_W1 = SETUP_V_SHIFT + 5

        def over_tiles(rows, g):
            batch = g.batch
            row = rows[:, batch:batch + 1, :] if isinstance(batch, int) else rows[:, bass.ds(batch, 1), :]
            return row.broadcast_to([P, TILES, P])

        def mod_col(which, g):
            batch = g.batch
            if isinstance(batch, int):
                return mod_cols[:, which, batch:batch + 1]
            return mod_cols[:, which, bass.ds(batch, 1)]

        def x2_of(g, first=0, width=TOK):
            start = (g.batch % 2) * (2 * TOK) + (g.slot * TOK + first)
            return x2_tm[:, start:start + width] if isinstance(start, int) else x2_tm[:, bass.ds(start, width)]

        def settle(engine):
            engine.nop(nofuse=True)

        def by_tile(rows):
            return rows.rearrange("p (t c) -> p t c", t=TILES)

        @block.sync
        def _(sp):
            def load_x(g):
                if exists(g - 2):
                    sp.wait_ge(n1_done, nth(g - 2, 1, 1))
                    settle(sp)
                    sp.wait_ge(xb_done, nth(g - 2, 1, 1))
                settle(sp)
                sp.dma_start(x_tm[:, g.slot, :], x[g.number]).then_inc(x_loaded[g.slot], 16)

            sp.dma_start(c_sb[:], cT).then_inc(s_weights["c"], 16)
            load_x(Group(0, 0))
            sp.dma_start(wmod_sb[:], wmod).then_inc(s_weights["wmod"], 16)
            sp.dma_start(wbeta_sb[:], wbeta).then_inc(s_weights["wbeta"], 16)
            sp.dma_start(wv_sb[:], wv).then_inc(s_weights["wv"], 16)
            sp.dma_start(attn_w[:, K, :], wk).then_inc(s_weights["wk"], 16)
            sp.dma_start(wq_sb[:], wq).then_inc(s_weights["wq"], 16)
            sp.dma_start(attn_w[:, OUT, :], wo).then_inc(s_weights["wo"], 16)
            load_x(Group(0, 1))
            sp.dma_start(w1[:], w1T).then_inc(s_weights["w1"], 16)
            sp.dma_start(w2[:], w2T).then_inc(s_weights["w2"], 16)

            def slot(s, experts, late, early):
                if s == 0 and late:
                    pass
                if s == 4 and early is not None and not (isinstance(early.b, int) and early.number < 1):
                    nxt = early + 1
                    if not (isinstance(nxt.b, int) and nxt.number >= GROUPS):
                        load_x(nxt)
                if s == 7 and late:
                    sp.wait_ge(comb_em_done, nth(late, 1, 1))
                    settle(sp)
                    if exists(late - 1):
                        sp.wait_ge(comb_spread, nth(late - 1, E, E))
                        settle(sp)
                    sp.dma_start(comb_row[0:1, :], comb_em[:]).then_inc(row_loaded, 16)
                if s == 7 and experts and exists(experts - 1):
                    store(experts - 1)

            def store(g):
                sp.wait_ge(out_done, nth(g, 1, 1))
                settle(sp)
                sp.dma_start(out[g.number], out_tm[:, g.slot, :]).then_inc(stored[g.slot], 16)

            run(sp, slot)
            store(Group(BATCHES - 1, 1))
            for p in range(2):
                sp.wait_ge(stored[p], 16 * BATCHES)

        @block.gpsimd
        def _(pool):
            nc.gpsimd.memset(ident[:], 0.0).then_inc(ident_zero, 1)
            pool.wait_ge(ident_zero, 1)
            nc.gpsimd.affine_select(out=ident[:], in_=ident[:], compare_op=ALU.not_equal, fill=1.0, base=0,
                                    pattern=[[-1, P]], channel_multiplier=1).then_inc(consts, 1)
            nc.gpsimd.memset(minus_half[:], -0.5).then_inc(consts, 1)
            nc.gpsimd.iota(expert_ids[:], pattern=[[0, TILES], [1, E]], base=0, channel_multiplier=0,
                           allow_small_or_imprecise_dtypes=True).then_inc(consts, 1)
            pool.wait_ge(consts, 3)

            def rstd(g, mv, mv_done, ve, ve_done, r, r_done, r_used):
                pool.wait_ge(mv_done, nth(g, 1, 1))
                settle(pool)
                nc.gpsimd.tensor_scalar(ve[:], mv[:, :, 1], 1.0, EPS, ALU.mult, ALU.add).then_inc(ve_done, 1)
                pool.wait_ge(ve_done, nth(g, 1, 1))
                if exists(g - 1):
                    pool.wait_ge(r_used, nth(g - 1, 1, 1))
                nc.gpsimd.tensor_tensor(r[:], ve[:], minus_half[:], ALU.pow).then_inc(r_done, 1)

            def spread(g, e):
                if e == 0:
                    pool.wait_ge(row_loaded, nth(g, 16, 16))
                if e >= 4:
                    pool.wait_ge(scaled_done, nth(g, E, e - 3))
                elif exists(g - 1):
                    pool.wait_ge(scaled_done, nth(g - 1, E, e + 5))
                settle(pool)
                nc.gpsimd.partition_broadcast(comb_cm[:, e % 4, :], comb_row[0:1, e * TOK:(e + 1) * TOK], P)\
                    .then_inc(comb_spread, 1)

            def add_expert(g, e):
                pool.wait_ge(scaled_done, nth(g, E, e + 1))
                if e >= 2:
                    pool.wait_ge(sum_done, nth(g, E - 1, e - 1))
                nc.gpsimd.tensor_tensor(sum_cm[:, g.slot, :], sum_cm[:, g.slot, :], scaled_cm[:, e % 2, :], ALU.add)\
                    .then_inc(sum_done, 1)

            def slot(s, experts, late, early):
                if experts:
                    if s >= 2:
                        add_expert(experts, s - 1)
                    elif s == 0 and exists(experts - 1):
                        add_expert(experts - 1, E - 1)
                    if s < 6:
                        spread(experts, s + 2)
                if late:
                    if s == 0:
                        rstd(late, lnz_mv, lnz_mv_done, lnz_ve, lnz_ve_done, lnz_r, lnz_r_done, nz_done)
                    if s == 2:
                        rstd(late, ln2_mv, ln2_mv_done, ln2_ve, ln2_ve_done, ln2_r, ln2_r_done, n2_done)
                    if s == 3:
                        rstd(late, ln3_mv, ln3_mv_done, ln3_ve, ln3_ve_done, ln3_r, ln3_r_done, rn_done)
                    if s == 7:
                        spread(late, 0)
                        spread(late, 1)
                if early:
                    if s == 0 and not exists(early - 1):
                        rstd(early, ln1_mv, ln1_mv_done, ln1_ve, ln1_ve_done, ln1_r, ln1_r_done, n1_done)
                    if s == 1:
                        if early.k == 0 and isinstance(early.b, int) and early.b == 0:
                            pool.wait_ge(setup_v, SETUP_V_SHIFT)
                        pool.wait_ge(x_loaded[early.slot], turn(early))
                        if exists(early - 2):
                            pool.wait_ge(x2_done, nth(early - 2, 1, 1))
                        xv = x_tm[:, early.slot, :].rearrange("p (t c) -> p t c", t=TILES)
                        xb = xb_tm[:, early.slot, :].rearrange("p (t c) -> p t c", t=TILES)
                        settle(pool)
                        nc.gpsimd.tensor_tensor(xb, xv, over_tiles(shift_a, early), ALU.add).then_inc(xb_done, 1)
                    if s == 7:
                        nxt = early + 1
                        if not (isinstance(nxt.b, int) and nxt.number >= GROUPS):
                            rstd(nxt, ln1_mv, ln1_mv_done, ln1_ve, ln1_ve_done, ln1_r, ln1_r_done, n1_done)

            run(pool, slot)
            add_expert(Group(BATCHES - 1, 1), E - 1)

        @block.scalar
        def _(act):
            act.dma_start(cols[:, 0:1], b_beta.rearrange("(h o) -> h o", o=1).broadcast_to([HEADS, D]))\
                .then_inc(s_weights["cols"], 16)
            act.dma_start(cols[:, 1:2], b_o.rearrange("(c o) -> c o", o=1)).then_inc(s_weights["cols"], 16)
            act.dma_start(cols[:, 2:3], gamma.rearrange("(c o) -> c o", o=1)).then_inc(s_weights["cols"], 16)
            act.dma_start(cols[:, 3:4], beta_.rearrange("(c o) -> c o", o=1)).then_inc(s_weights["cols"], 16)
            act.dma_start(lng_rows[:], ln_g.rearrange("(o c) -> o c", o=1).broadcast_to([P, P]))\
                .then_inc(s_weights["rows"], 16)
            act.dma_start(lnb_rows[:], ln_b.rearrange("(o c) -> o c", o=1).broadcast_to([P, P]))\
                .then_inc(s_weights["rows"], 16)
            act.dma_start(gate[:], gateT).then_inc(s_weights["gate"], 16)
            act.wait_ge(s_weights["c"], 16)
            nc.scalar.activation(c_tanh[:], c_sb[:], ACT.Tanh, scale=0.5).then_inc(setup_a, 1)

            def gelu(g, e):
                act.wait_ge(up_done, nth(g, E, e + 1))
                if e >= 2:
                    act.wait_ge(down_done, nth(g, E, e - 1))
                elif exists(g - 1):
                    act.wait_ge(down_done, nth(g - 1, E, e + 7))
                nc.scalar.activation(gelu_cm[:, e % 2, :, :], up_ps[:, e % 2, :, :], ACT.Gelu).then_inc(gelu_done, 1)

            def slot(s, experts, late, early):
                if experts and s < 7:
                    gelu(experts, s + 1)
                if s == 7 and late:
                    gelu(late, 0)
                if s == 5 and experts and exists(experts - 1):
                    gate_sum(experts - 1)
                if early:
                    if s == 1:
                        act.wait_ge(n1_turned, nth(early, 1, 1))
                        if early.k == 0 and isinstance(early.b, int) and early.b == 0:
                            act.wait_ge(setup_v, SETUP_V_COLS)
                        if exists(early - 1):
                            act.wait_ge(z_done, nth(early - 1, 1, 1))
                        settle(act)
                        nc.scalar.activation(h_cm[:], ps1[:], ACT.Identity, scale=mod_col(1, early),
                                             bias=mod_col(0, early)).then_inc(h_done, 1)
                        act.wait_ge(h_done, nth(early, 1, 1))
                        if exists(early - 1):
                            act.wait_ge(q_ps_done, nth(early - 1, 1, 1))
                        nc.scalar.activation(h_hi[:], h_cm[:], ACT.Copy).then_inc(h_hi_done, 1)
                    if s == 2:
                        act.wait_ge(beta_ps_done, nth(early, 1, 1))
                        if early.k == 0 and isinstance(early.b, int) and early.b == 0:
                            act.wait_ge(setup_v, SETUP_V_HALF)
                        if exists(early - 1):
                            act.wait_ge(beta_done, nth(early - 1, 1, 1))
                        nc.scalar.activation(beta_tanh[:], ps1[:], ACT.Tanh, scale=0.5, bias=half_b_beta[:])\
                            .then_inc(beta_tanh_done, 1)
                        act.wait_ge(v_ps_done, nth(early, 1, 1))
                        if exists(early - 1):
                            act.wait_ge(kv_done, nth(early - 1, 1, 1))
                        nc.scalar.activation(vsum_cm[:], ps0[:], ACT.Copy).then_inc(vsum_done, 1)
                    if s == 5:
                        act.wait_ge(o_done, nth(early, 1, 1))
                        if exists(early - 1):
                            act.wait_ge(out_ps_done, nth(early - 1, 1, 1))
                        nc.scalar.activation(o_hi[:], o_cm[:], ACT.Copy).then_inc(o_hi_done, 1)
                if late:
                    if s == 4:
                        act.wait_ge(rn_turned, nth(late, 1, 1))
                        if exists(late - 1):
                            act.wait_ge(logits_ps_done, nth(late - 1, 1, 1))
                        elif late.b == 0:
                            act.wait_ge(s_weights["cols"], 64)
                        nc.scalar.activation(rn_cm[:], ps2[:], ACT.Identity, scale=cols[:, 2:3], bias=cols[:, 3:4])\
                            .then_inc(rn_cm_done, 1)
                    if s == 6:
                        act.wait_ge(below_done, nth(late, 1, 1))
                        if exists(late - 1):
                            act.wait_ge(root_done, nth(late - 1, 1, 1))
                        nc.scalar.activation(exp_tanh[:], below[:], ACT.Tanh, scale=0.5 / 2 ** EXP_SQUARINGS)\
                            .then_inc(exp_tanh_done, 1)
                        act.wait_ge(h2_turned, nth(late, 1, 1))
                        if exists(late - 2):
                            act.wait_ge(up_done, nth(late - 2, E, E))
                        nc.scalar.activation(h2_hi[:, late.slot, :], ps2[:], ACT.Copy).then_inc(h2_hi_done, 1)
                        act.wait_ge(root_done, nth(late, 1, 1))
                        for n in range(EXP_SQUARINGS):
                            if n:
                                act.wait_ge(squared, nth(late, EXP_SQUARINGS, n))
                            elif exists(late - 1):
                                act.wait_ge(exp_sum_done, nth(late - 1, 1, 1))
                            nc.scalar.activation(powers[:, n + 1], powers[:, n], ACT.Square).then_inc(squared, 1)
                    if s == 7:
                        act.wait_ge(comb_turned, nth(late, 1, 1))
                        if exists(late - 1):
                            act.wait_ge(row_loaded, nth(late - 1, 16, 16))
                        nc.scalar.activation(comb_em[:], ps2[0:E * TILES, 0:P], ACT.Copy).then_inc(comb_em_done, 1)

            def gate_sum(g):
                act.wait_ge(sum_done, nth(g, E - 1, E - 1))
                if exists(g - 1):
                    act.wait_ge(gated_turned, nth(g - 1, 1, 1))
                settle(act)
                nc.scalar.activation(gated_cm[:], sum_cm[:, g.slot, :], ACT.Copy, scale=mod_col(2, g))\
                    .then_inc(gated_done, 1)

            run(act, slot)
            gate_sum(Group(BATCHES - 1, 1))

        @block.vector
        def _(dve):
            done = [0]

            def then(ins):
                done[0] += 1
                ins.then_inc(setup_v, 1)
                dve.wait_ge(setup_v, done[0])

            def split(which, hi, lo):
                then(nc.vector.tensor_copy(hi, which))
                then(nc.vector.tensor_tensor(lo, which, hi.bitcast(F32), ALU.subtract))

            def ln_stats(dve, g):
                dve.wait_ge(x_loaded[0], 16)
                for t in range(TILES):
                    ins = nc.vector.bn_stats(ln1_bn[:, t, :], x_tm[:, 0, tile(t)])
                ins.then_inc(ln1_bn_done, 1)
                dve.wait_ge(ln1_bn_done, 1)
                settle(dve)
                for t in range(TILES):
                    ins = nc.vector.bn_aggr(ln1_mv[:, t, :], ln1_bn[:, t, :])
                ins.then_inc(ln1_mv_done, 1)

            dve.wait_ge(setup_a, 1)
            then(nc.vector.tensor_scalar(c_sig[:], c_tanh[:], 0.5, 0.5, ALU.mult, ALU.add))
            then(nc.vector.tensor_tensor(silu_c[:], c_sb[:], c_sig[:], ALU.mult))
            then(nc.vector.tensor_copy(silu_rows[:], silu_c[:].rearrange("p (b o) -> p b o", o=1)
                                       .broadcast_to([P, BATCHES, P])))
            assert done[0] == SETUP_V_SILU

            def clamp(dst, g, width):
                sign, size = gate_sign[:, 0:width], gate_abs[:, 0:width]
                then(nc.vector.tensor_scalar(sign, g, 0.0, 2.0, ALU.is_ge, ALU.mult))
                then(nc.vector.tensor_scalar(sign, sign, -1.0, None, ALU.add))
                then(nc.vector.tensor_tensor(size, g, sign, ALU.mult))
                then(nc.vector.scalar_tensor_tensor(out=dst, in0=size, scalar=GATE_FLOOR, in1=sign,
                                                    op0=ALU.max, op1=ALU.mult))

            dve.wait_ge(setup_p, 1)
            then(nc.vector.tensor_copy(mod_cols[:, 0, :], ps0[:, 0:BATCHES]))
            then(nc.vector.tensor_scalar(mod_cols[:, 1, :], ps0[:, BATCHES:2 * BATCHES], 1.0, None, ALU.add))
            ln_stats(dve, Group(0, 0))
            then(nc.vector.tensor_copy(mod_cols[:, 2, :], ps0[:, 2 * BATCHES:3 * BATCHES]))
            assert done[0] == SETUP_V_COLS
            dve.wait_ge(s_weights["cols"], 64)
            then(nc.vector.tensor_scalar(half_b_beta[:], cols[:, 0:1], 0.5, None, ALU.mult))
            assert done[0] == SETUP_V_HALF
            dve.wait_ge(s_weights["wbeta"], 16)

            def by_head(row):
                return row.rearrange("p (h d) -> p h d", h=HEADS)

            def repeated(row):
                return row.rearrange("p (h o) -> p h o", o=1).broadcast_to([P, HEADS, D])

            then(nc.vector.tensor_copy(by_head(attn_w[:, BETA, :]), repeated(wbeta_sb[:])))
            split(attn_w[:, BETA, :], attn_hi[:, BETA, :], attn_lo[:, BETA, :])
            assert done[0] == SETUP_V_BETA
            dve.wait_ge(s_weights["wv"], 16)
            then(nc.vector.tensor_reduce(head_sums[:, 0, :], by_head(wv_sb[:]), AX_X, ALU.add))
            then(nc.vector.tensor_copy(by_head(attn_w[:, V, :]), repeated(head_sums[:, 0, :])))
            split(attn_w[:, V, :], attn_hi[:, V, :], attn_lo[:, V, :])
            assert done[0] == SETUP_V_V
            dve.wait_ge(s_weights["wk"], 16)
            split(attn_w[:, K, :], attn_hi[:, K, :], attn_lo[:, K, :])
            assert done[0] == SETUP_V_K
            dve.wait_ge(s_weights["wq"], 16)
            then(nc.vector.tensor_reduce(head_sums[:, 1, :], by_head(wq_sb[:]), AX_X, ALU.add))
            then(nc.vector.tensor_copy(by_head(attn_w[:, Q, :]), repeated(head_sums[:, 1, :])))
            split(attn_w[:, Q, :], attn_hi[:, Q, :], attn_lo[:, Q, :])
            assert done[0] == SETUP_V_Q
            dve.wait_ge(s_weights["wo"], 16)
            split(attn_w[:, OUT, :], attn_hi[:, OUT, :], attn_lo[:, OUT, :])
            assert done[0] == SETUP_V_OUT
            dve.wait_ge(s_weights["rows"], 32)
            for b in range(BATCHES):
                rows = down_ps if b % 2 else ps2
                dve.wait_ge(setup_p, 2 + b)
                clamp(ga_rows[:], rows[:, 0:P], P)
                then(nc.vector.tensor_tensor(scale_a[:, b, :], ga_rows[:], lng_rows[:], ALU.mult))
                then(nc.vector.tensor_tensor(shift_a[:, b, :], ga_rows[:], lnb_rows[:], ALU.mult))
                then(nc.vector.tensor_copy(shift_b[:, b, :], rows[:, P:2 * P]))
                then(nc.vector.tensor_scalar(scale_b[:, b, :], rows[:, 2 * P:3 * P], 1.0, None, ALU.add))
            assert done[0] == SETUP_V_SHIFT
            clamp(mod_cols[:, 2, :], mod_cols[:, 2, :], BATCHES)
            dve.wait_ge(s_weights["w1"], 16)
            then(nc.vector.tensor_copy(w1_hi[:], w1[:]))
            assert done[0] == SETUP_V_W1
            then(nc.vector.tensor_tensor(w1_lo[:], w1[:], w1_hi[:].bitcast(F32), ALU.subtract))
            assert done[0] == SETUP_V_W1 + 1
            dve.wait_ge(consts, 3)

            def stats(g, src, bn, bn_done, mv, mv_done, mv_used):
                settle(dve)
                for t in range(TILES):
                    ins = nc.vector.bn_stats(bn[:, t, :], src(t))
                ins.then_inc(bn_done, 1)
                dve.wait_ge(bn_done, nth(g, 1, 1))
                if exists(g - 1):
                    dve.wait_ge(mv_used, nth(g - 1, 1, 1))
                settle(dve)
                for t in range(TILES):
                    ins = nc.vector.bn_aggr(mv[:, t, :], bn[:, t, :])
                ins.then_inc(mv_done, 1)

            def normalize(dst, src, mv, r, n_done):
                for t in range(TILES):
                    ins = nc.vector.tensor_scalar(dst[:, tile(t)], src(t), mv[:, t, 0:1], r[:, t:t + 1],
                                                  ALU.subtract, ALU.mult)
                ins.then_inc(n_done, 1)

            def scale_expert(g, e):
                dve.wait_ge(down_done, nth(g, E, e + 1))
                dve.wait_ge(comb_spread, nth(g, E, e + 1))
                if e == 0:
                    if exists(g - 2):
                        dve.wait_ge(gated_done, nth(g - 2, 1, 1))
                    dst = sum_cm[:, g.slot, :]
                else:
                    if e >= 3:
                        dve.wait_ge(sum_done, nth(g, E - 1, e - 2))
                    elif exists(g - 1):
                        dve.wait_ge(sum_done, nth(g - 1, E - 1, 6 if e == 2 else 7))
                    dst = scaled_cm[:, e % 2, :]
                nc.vector.tensor_tensor(dst, down_ps[:], comb_cm[:, e % 4, :], ALU.mult).then_inc(scaled_done, 1)

            def add_residual(g):
                dve.wait_ge(gated_turned, nth(g, 1, 1))
                if exists(g - 2):
                    dve.wait_ge(stored[g.slot], turn(g - 2))
                nc.vector.tensor_tensor(out_tm[:, g.slot, :], ps0[:], x2_of(g), ALU.add)\
                    .then_inc(out_done, 1)

            def slot(s, experts, late, early):
                if early and s == 2:
                    dve.wait_ge(h_hi_done, nth(early, 1, 1))
                    nc.vector.tensor_tensor(h_lo[:], h_cm[:], h_hi[:].bitcast(F32), ALU.subtract).then_inc(h_lo_done, 1)
                if experts:
                    if s:
                        scale_expert(experts, s - 1)
                    elif exists(experts - 1):
                        scale_expert(experts - 1, E - 1)
                if s == 0:
                    if early:
                        dve.wait_ge(ln1_r_done, nth(early, 1, 1))
                        if exists(early - 1):
                            dve.wait_ge(n1_turned, nth(early - 1, 1, 1))
                        normalize(n1_tm, tiles_of(x_tm[:, early.slot, :]), ln1_mv, ln1_r, n1_done)
                    if late:
                        dve.wait_ge(z_turned, nth(late, 1, 1))
                        stats(late, tiles_of(ps0), lnz_bn, lnz_bn_done, lnz_mv, lnz_mv_done, nz_done)
                if s == 1 and late:
                    dve.wait_ge(lnz_r_done, nth(late, 1, 1))
                    normalize(nz_tm, tiles_of(ps0), lnz_mv, lnz_r, nz_done)
                    dve.wait_ge(nz_done, nth(late, 1, 1))
                    nc.vector.tensor_tensor(by_tile(nza_tm[:]), by_tile(nz_tm[:]), over_tiles(scale_a, late), ALU.mult)\
                        .then_inc(nza_done, 1)
                    dve.wait_ge(nza_done, nth(late, 1, 1))
                    dve.wait_ge(xb_done, nth(late, 1, 1))
                    nc.vector.tensor_tensor(x2_of(late), nza_tm[:], xb_tm[:, late.slot, :], ALU.add)\
                        .then_inc(x2_done, 1)
                if s == 2 and late:
                    dve.wait_ge(x2_done, nth(late, 1, 1))
                    stats(late, lambda t: x2_of(late, t * P, P), ln2_bn, ln2_bn_done, ln2_mv, ln2_mv_done, n2_done)
                if s == 3 and late:
                    dve.wait_ge(ln2_r_done, nth(late, 1, 1))
                    normalize(n2_tm, lambda t: x2_of(late, t * P, P), ln2_mv, ln2_r, n2_done)
                    dve.wait_ge(n2_done, nth(late, 1, 1))
                    nc.vector.tensor_tensor(by_tile(n2c_tm[:]), by_tile(n2_tm[:]), over_tiles(scale_b, late), ALU.mult)\
                        .then_inc(n2c_done, 1)
                    dve.wait_ge(n2c_done, nth(late, 1, 1))
                    if exists(late - 1):
                        dve.wait_ge(h2_turned, nth(late - 1, 1, 1))
                    nc.vector.tensor_tensor(by_tile(h2_tm[:]), by_tile(n2c_tm[:]), over_tiles(shift_b, late), ALU.add)\
                        .then_inc(h2_done, 1)
                    dve.wait_ge(h2_done, nth(late, 1, 1))
                    stats(late, tiles_of(h2_tm), ln3_bn, ln3_bn_done, ln3_mv, ln3_mv_done, rn_done)
                if s == 4:
                    if early:
                        dve.wait_ge(beta_tanh_done, nth(early, 1, 1))
                        if exists(early - 1):
                            dve.wait_ge(scan_done, nth(early - 1, 1, 1))
                        nc.vector.tensor_scalar(beta_cm[:], beta_tanh[:], 0.5, 0.5, ALU.mult, ALU.add)\
                            .then_inc(beta_done, 1)
                        dve.wait_ge(k_ps_done, nth(early, 1, 1))
                        dve.wait_ge(vsum_done, nth(early, 1, 1))
                        nc.vector.tensor_tensor(kv_cm[:], ps1[:], vsum_cm[:], ALU.mult).then_inc(kv_done, 1)
                    if late:
                        dve.wait_ge(ln3_r_done, nth(late, 1, 1))
                        if exists(late - 1):
                            dve.wait_ge(rn_turned, nth(late - 1, 1, 1))
                        normalize(rn_tm, tiles_of(h2_tm), ln3_mv, ln3_r, rn_done)
                    if early:
                        dve.wait_ge(beta_done, nth(early, 1, 1))
                        dve.wait_ge(kv_done, nth(early, 1, 1))
                        if exists(early - 2):
                            dve.wait_ge(o_done, nth(early - 2, 1, 1))
                        start = 0.0 if early.slot == 0 else state_cm[:, 0, TOK - 1:TOK]
                        nc.vector.tensor_tensor_scan(state_cm[:, early.slot, :], beta_cm[:], kv_cm[:], start,
                                                     ALU.mult, ALU.add).then_inc(scan_done, 1)
                if s == 5:
                    if early:
                        dve.wait_ge(scan_done, nth(early, 1, 1))
                        dve.wait_ge(q_ps_done, nth(early, 1, 1))
                        if exists(early - 1):
                            dve.wait_ge(o_lo_done, nth(early - 1, 1, 1))
                        nc.vector.tensor_tensor(o_cm[:], ps0[:], state_cm[:, early.slot, :], ALU.mult)\
                            .then_inc(o_done, 1)
                    if late:
                        dve.wait_ge(logits_ps_done, nth(late, 1, 1))
                        nc.vector.tensor_copy(logits[:], ps2[:, 0:TILES * E].rearrange("p (t e) -> p t e", e=E))\
                            .then_inc(logits_done, 1)
                        dve.wait_ge(logits_done, nth(late, 1, 1))
                        settle(dve)
                        for t in range(TILES):
                            ins = nc.vector.max(top[:, t, :], logits[:, t, :])
                        ins.then_inc(top_done, 1)
                    if early:
                        dve.wait_ge(o_hi_done, nth(early, 1, 1))
                        nc.vector.tensor_tensor(o_lo[:], o_cm[:], o_hi[:].bitcast(F32), ALU.subtract)\
                            .then_inc(o_lo_done, 1)
                    if late:
                        dve.wait_ge(top_done, nth(late, 1, 1))
                        nc.vector.tensor_tensor(below[:], logits[:], top[:, :, 0:1].broadcast_to([P, TILES, E]),
                                                ALU.subtract).then_inc(below_done, 1)
                if s == 6 and late:
                    for t in range(TILES):
                        ins = nc.vector.max_index(top_ids[:, t, :], top[:, t, :], logits[:, t, :])
                    ins.then_inc(top_ids_done, 1)
                    dve.wait_ge(exp_tanh_done, nth(late, 1, 1))
                    nc.vector.tensor_scalar(exp_den[:], exp_tanh[:], -1.0, 1.0, ALU.mult, ALU.add).then_inc(den_done, 1)
                    dve.wait_ge(top_ids_done, nth(late, 1, 1))
                    nc.vector.tensor_tensor(is_first[:], expert_ids[:], top_ids[:, :, 0:1].broadcast_to([P, TILES, E]),
                                            ALU.is_equal)
                    nc.vector.tensor_tensor(is_second[:], expert_ids[:], top_ids[:, :, 1:2].broadcast_to([P, TILES, E]),
                                            ALU.is_equal).then_inc(is_top_done, 1)
                    dve.wait_ge(den_done, nth(late, 1, 1))
                    nc.vector.reciprocal(exp_rec[:], exp_den[:]).then_inc(rec_done, 1)
                    dve.wait_ge(is_top_done, nth(late, 1, 1))
                    nc.vector.tensor_tensor(chosen[:], is_first[:], is_second[:], ALU.add).then_inc(chosen_done, 1)
                    dve.wait_ge(rec_done, nth(late, 1, 1))
                    if exists(late - 1):
                        dve.wait_ge(squared, nth(late - 1, EXP_SQUARINGS, 1))
                    nc.vector.scalar_tensor_tensor(out=powers[:, 0], in0=exp_tanh[:], scalar=1.0, in1=exp_rec[:],
                                                   op0=ALU.add, op1=ALU.mult).then_inc(root_done, 1)
                    dve.wait_ge(h2_hi_done, nth(late, 1, 1))
                    nc.vector.tensor_tensor(h2_lo[:, late.slot, :], ps2[:], h2_hi[:, late.slot, :].bitcast(F32),
                                            ALU.subtract).then_inc(h2_lo_done, 1)
                    dve.wait_ge(squared, nth(late, EXP_SQUARINGS, EXP_SQUARINGS))
                    dve.wait_ge(chosen_done, nth(late, 1, 1))
                    nc.vector.tensor_tensor(exp_chosen[:], powers[:, EXP_SQUARINGS], chosen[:], ALU.mult)\
                        .then_inc(exp_chosen_done, 1)
                    nc.vector.tensor_reduce(exp_sum[:], powers[:, EXP_SQUARINGS], AX_X, ALU.add)\
                        .then_inc(exp_sum_done, 1)
                    dve.wait_ge(exp_sum_done, nth(late, 1, 1))
                    nc.vector.reciprocal(exp_sum_rec[:], exp_sum[:]).then_inc(exp_sum_rec_done, 1)
                    dve.wait_ge(exp_sum_rec_done, nth(late, 1, 1))
                    dve.wait_ge(exp_chosen_done, nth(late, 1, 1))
                    if exists(late - 1):
                        dve.wait_ge(comb_turned, nth(late - 1, 1, 1))
                    nc.vector.tensor_tensor(comb_tm[:].rearrange("p e t -> p t e"), exp_chosen[:],
                                            exp_sum_rec[:].rearrange("p (t o) -> p t o", o=1)
                                            .broadcast_to([P, TILES, E]), ALU.mult).then_inc(comb_done, 1)
                if s == 7:
                    if experts and exists(experts - 1):
                        add_residual(experts - 1)
                    if early:
                        dve.wait_ge(out_ps_done, nth(early, 1, 1))
                        if exists(early - 1):
                            dve.wait_ge(z_turned, nth(early - 1, 1, 1))
                        nc.vector.scalar_tensor_tensor(out=z_cm[:], in0=ps1[:], scalar=cols[:, 1:2], in1=h_cm[:],
                                                       op0=ALU.add, op1=ALU.add).then_inc(z_done, 1)
                        nxt = early + 1
                        if not (isinstance(nxt.b, int) and nxt.number >= GROUPS):
                            dve.wait_ge(x_loaded[nxt.slot], turn(nxt))
                            stats(nxt, tiles_of(x_tm[:, nxt.slot, :]), ln1_bn, ln1_bn_done, ln1_mv, ln1_mv_done, n1_done)

            run(dve, slot)
            scale_expert(Group(BATCHES - 1, 1), E - 1)
            add_residual(Group(BATCHES - 1, 1))

        @block.tensor
        def _(pe):
            SA, CA, GA, SB, CB, GB = (slice(j * P, (j + 1) * P) for j in range(6))
            pe.wait_ge(s_weights["wmod"], 16)
            pe.wait_ge(setup_v, SETUP_V_SILU)
            for n, part in enumerate((SA, CA, GB)):
                ins = nc.tensor.matmul(ps0[:, n * BATCHES:(n + 1) * BATCHES], wmod_sb[:, part], silu_c[:],
                                       start=True, stop=True)
            ins.then_inc(setup_p, 1)
            for b in range(BATCHES):
                rows = down_ps if b % 2 else ps2
                if b >= 2:
                    pe.wait_ge(setup_v, SETUP_V_OUT + 8 * (b - 1))
                nc.tensor.matmul(rows[:, 0:3 * P], silu_rows[:, b, :], wmod_sb[:, 2 * P:5 * P],
                                 start=True, stop=True).then_inc(setup_p, 1)

            def product(dst, w_hi, w_lo, x_hi, x_lo, start=True, stop=True):
                nc.tensor.matmul(dst, w_hi, x_hi, start=start, stop=False)
                nc.tensor.matmul(dst, w_lo, x_hi, start=False, stop=False)
                return nc.tensor.matmul(dst, w_hi, x_lo, start=False, stop=stop)

            def turn_tiles(dst, src):
                for t in range(TILES):
                    ins = nc.tensor.transpose(dst[:, tile(t)], src[:, tile(t)], ident[:])
                return ins

            def project(dst, which, x_hi, x_lo):
                return product(dst, attn_hi[:, which, :], attn_lo[:, which, :], x_hi[:], x_lo[:])

            def up(g, e):
                if e >= 2:
                    pe.wait_ge(gelu_done, nth(g, E, e - 1))
                elif exists(g - 1):
                    pe.wait_ge(gelu_done, nth(g - 1, E, e + 7))
                if e == 0:
                    pe.wait_ge(h2_hi_done, nth(g, 1, 1))
                    pe.wait_ge(h2_lo_done, nth(g, 1, 1))
                for f in range(2):
                    w = slice(e * 256 + f * P, e * 256 + (f + 1) * P)
                    ins = product(up_ps[:, e % 2, f, :], w1_hi[:, w], w1_lo[:, w],
                                  h2_hi[:, g.slot, :], h2_lo[:, g.slot, :])
                ins.then_inc(up_done, 1)

            def down(g, e):
                pe.wait_ge(gelu_done, nth(g, E, e + 1))
                if e:
                    pe.wait_ge(scaled_done, nth(g, E, e))
                elif exists(g - 1):
                    pe.wait_ge(scaled_done, nth(g - 1, E, E))
                for f in range(2):
                    ins = nc.tensor.matmul(down_ps[:], w2[:, e, f, :], gelu_cm[:, e % 2, f, :],
                                           start=(f == 0), stop=(f == 1))
                ins.then_inc(down_done, 1)

            def turn_gated(g):
                pe.wait_ge(gated_done, nth(g, 1, 1))
                turn_tiles(ps0, gated_cm).then_inc(gated_turned, 1)

            def slot(s, experts, late, early):
                if experts and s < 7:
                    up(experts, s + 1)
                if s == 7 and late:
                    if not exists(late - 1):
                        pe.wait_ge(setup_v, SETUP_V_W1 + 1)
                    up(late, 0)
                if s == 0 and late:
                    pe.wait_ge(z_done, nth(late, 1, 1))
                    turn_tiles(ps0, z_cm).then_inc(z_turned, 1)
                if s == 1 and early:
                    pe.wait_ge(n1_done, nth(early, 1, 1))
                    if not exists(early - 1):
                        pe.wait_ge(consts, 3)
                    turn_tiles(ps1, n1_tm).then_inc(n1_turned, 1)
                if s == 2 and early:
                    if not exists(early - 1):
                        pe.wait_ge(setup_v, SETUP_V_OUT)
                    pe.wait_ge(h_hi_done, nth(early, 1, 1))
                    pe.wait_ge(h_lo_done, nth(early, 1, 1))
                    project(ps1[:], BETA, h_hi, h_lo).then_inc(beta_ps_done, 1)
                    if late:
                        pe.wait_ge(nz_done, nth(late, 1, 1))
                    project(ps0[:], V, h_hi, h_lo).then_inc(v_ps_done, 1)
                if s == 3 and early:
                    pe.wait_ge(beta_tanh_done, nth(early, 1, 1))
                    project(ps1[:], K, h_hi, h_lo).then_inc(k_ps_done, 1)
                    pe.wait_ge(vsum_done, nth(early, 1, 1))
                    project(ps0[:], Q, h_hi, h_lo).then_inc(q_ps_done, 1)
                if s == 4 and late:
                    pe.wait_ge(rn_done, nth(late, 1, 1))
                    turn_tiles(ps2, rn_tm).then_inc(rn_turned, 1)
                if s == 5 and late:
                    pe.wait_ge(rn_cm_done, nth(late, 1, 1))
                    if not exists(late - 1):
                        pe.wait_ge(s_weights["gate"], 16)
                    for t in range(TILES):
                        ins = nc.tensor.matmul(ps2[:, t * E:(t + 1) * E], rn_cm[:, tile(t)], gate[:],
                                               start=True, stop=True)
                    ins.then_inc(logits_ps_done, 1)
                if s == 6:
                    if late:
                        pe.wait_ge(logits_done, nth(late, 1, 1))
                        turn_tiles(ps2, h2_tm).then_inc(h2_turned, 1)
                    if experts and exists(experts - 1):
                        if early:
                            pe.wait_ge(o_done, nth(early, 1, 1))
                        turn_gated(experts - 1)
                    if early:
                        pe.wait_ge(o_hi_done, nth(early, 1, 1))
                        pe.wait_ge(o_lo_done, nth(early, 1, 1))
                        pe.wait_ge(kv_done, nth(early, 1, 1))
                        project(ps1[:], OUT, o_hi, o_lo).then_inc(out_ps_done, 1)
                if s == 7 and late:
                    pe.wait_ge(comb_done, nth(late, 1, 1))
                    pe.wait_ge(h2_lo_done, nth(late, 1, 1))
                    nc.tensor.transpose(ps2[0:E * TILES, 0:P], comb_tm[:].rearrange("p e t -> p (e t)"), ident[:])\
                        .then_inc(comb_turned, 1)
                if experts:
                    if s == 0 and not exists(experts - 1):
                        pe.wait_ge(s_weights["w2"], 16)
                    down(experts, s)

            run(pe, slot)
            turn_gated(Group(BATCHES - 1, 1))


def kernel(**inputs):
    import numpy as np
    import concourse.bacc as bacc
    from concourse import mybir as mb
    from concourse.bass_utils import run_bass_kernel_spmd

    def a(name):
        return np.asarray(inputs["L0_" + name])

    x = a("attn_x")
    B, S, C = x.shape
    groups = B * S // TOK
    E, F, _ = a("ffn_w1").shape
    arrays = {
        "x": x.reshape(groups, TILES, P, C).transpose(0, 2, 1, 3).reshape(groups, P, TOK),
        "cT": a("c").T,
        "wmod": a("wmod"),
        "wq": a("attn_Wq"), "wk": a("attn_Wk"), "wv": a("attn_Wv"), "wbeta": a("attn_Wbeta"),
        "b_beta": a("attn_b_beta"), "wo": a("attn_Wo"), "b_o": a("attn_b_o"),
        "ln_g": a("attn_ln_g"), "ln_b": a("attn_ln_b"),
        "gamma": a("ffn_ln_gamma"), "beta_": a("ffn_ln_beta"),
        "gateT": a("ffn_gate_w").T,
        "w1T": a("ffn_w1").transpose(2, 0, 1).reshape(C, E * F),
        "w2T": a("ffn_w2").reshape(E, C, F // P, P).transpose(3, 0, 2, 1),
    }
    arrays = {n: np.ascontiguousarray(v) for n, v in arrays.items()}
    nc = bacc.Bacc("TRN2", target_bir_lowering=False, num_devices=1)
    args = [nc.dram_tensor("in_" + n, v.shape, mb.dt.from_np(v.dtype), kind="ExternalInput").ap()
            for n, v in arrays.items()]
    out = nc.dram_tensor("out", (groups, P, TOK), mb.dt.float32, kind="ExternalOutput").ap()
    adaln_moe_kernel(nc, *args, out)
    r = run_bass_kernel_spmd(nc, [{"in_" + n: v for n, v in arrays.items()}], core_ids=[0])
    got = r.results[0]["out"]
    return got.reshape(groups, P, TILES, C).transpose(0, 2, 1, 3).reshape(B, S, C)
```

```python
from contextlib import ExitStack

import concourse.bass as bass
from concourse import mybir

F32 = mybir.dt.float32
F32R = mybir.dt.float32r
U32 = mybir.dt.uint32
ALU = mybir.AluOpType
ACT = mybir.ActivationFunctionType
AX_X = mybir.AxisListType.X

P = 128
TILES = 4
TOK = TILES * P
EPS = 1e-5
GATE_FLOOR = 0.25
EXP_SQUARINGS = 2
SPLIT = (0, 1, 7)


class Group:

    def __init__(self, b, k):
        self.b, self.k = b, k

    def __add__(self, n):
        return Group(self.b, self.k + n)

    def __sub__(self, n):
        return Group(self.b, self.k - n)

    @property
    def slot(self):
        return self.k % 2

    @property
    def number(self):
        return 2 * self.b + self.k

    @property
    def batch(self):
        return self.b + self.k // 2


def exists(group):
    return not isinstance(group.b, int) or group.number >= 0


def nth(group, per, n):
    return (2 * per) * group.b + (per * group.k + n)


def turn(group, by=16):
    return by * group.b + by * (group.k // 2 + 1)


def adaln_moe_kernel(nc, x, cT, wmod, wq, wk, wv, wbeta, b_beta, wo, b_o, ln_g, ln_b, gamma, beta_, gateT,
                     w1T, w2T, out):
    GROUPS = x.shape[0]
    BATCHES = cT.shape[1]
    HEADS = wbeta.shape[1]
    D = P // HEADS
    E = gateT.shape[1]
    assert GROUPS == 2 * BATCHES and E == 8

    with ExitStack() as ctx:
        def sb(name, shape, dt=F32):
            return ctx.enter_context(nc.sbuf_tensor(name, shape, dt))

        def psum(name, shape):
            return ctx.enter_context(nc.psum_tensor(name, shape, F32))

        def sem(name):
            return ctx.enter_context(nc.semaphore(name))

        up_ps = psum("up_ps", [P, 3, TOK])
        down_ps = psum("down_ps", [P, 2, TOK])
        ps0 = psum("ps0", [P, TOK])
        ps1 = psum("ps1", [P, TOK])
        ps2 = psum("ps2", [P, TOK])

        ident = sb("ident", [P, P])
        minus_half = sb("minus_half", [P, TILES])
        expert_ids = sb("expert_ids", [P, TILES, E])
        w1 = sb("w1", [P, E * 256])
        w1_hi = sb("w1_hi", [P, E * 256], F32R)
        w1_lo = sb("w1_lo", [P, E * 256], F32R)
        w2 = sb("w2", [P, E, 2, P])
        w2_hi = sb("w2_hi", [P, E, 2, P], F32R)
        w2_lo = sb("w2_lo", [P, E, 2, P], F32R)
        attn_w = sb("attn_w", [P, 5, P])
        attn_hi = sb("attn_hi", [P, 5, P], F32R)
        attn_lo = sb("attn_lo", [P, 5, P], F32R)
        Q, K, V, BETA, OUT = range(5)
        wq_sb = sb("wq_sb", [P, P])
        wv_sb = sb("wv_sb", [P, P])
        wbeta_sb = sb("wbeta_sb", [P, HEADS])
        head_sums = sb("head_sums", [P, 2, HEADS])
        cols = sb("cols", [P, 6])
        half_b_beta = sb("half_b_beta", [P, 1])
        gate = sb("gate", [P, E])
        gate_gamma = sb("gate_gamma", [P, E])
        gate_mid = sb("gate_mid", [P, E])
        gate_hi = sb("gate_hi", [P, E], F32R)
        gate_lo = sb("gate_lo", [P, E], F32R)
        gate_bias = sb("gate_bias", [P, E])
        mean_w = sb("mean_w", [P, P])
        wmod_sb = sb("wmod_sb", [P, 6 * P])
        c_sb = sb("c_sb", [P, BATCHES])
        c_tanh = sb("c_tanh", [P, BATCHES])
        c_sig = sb("c_sig", [P, BATCHES])
        silu_c = sb("silu_c", [P, BATCHES])
        mods = sb("mods", [P, 6, BATCHES])
        sign = sb("sign", [P, 2, BATCHES])
        size = sb("size", [P, 2, BATCHES])
        gates = sb("gates", [P, 2, BATCHES])
        row_cols = sb("row_cols", [P, BATCHES, 4])
        scale_h = sb("scale_h", [P, BATCHES])
        rows = sb("rows", [P, BATCHES, 4, P])
        SCALE_A, SHIFT_A, SCALE_B, SHIFT_B = range(4)

        x_tm = sb("x_tm", [P, 2, TOK])
        ln1_bn = sb("ln1_bn", [P, TILES, 6])
        ln1_mv = sb("ln1_mv", [P, TILES, 2])
        ln1_ve = sb("ln1_ve", [P, TILES])
        ln1_r = sb("ln1_r", [P, TILES])
        ln1_neg = sb("ln1_neg", [P, TILES])
        ln1_nmr = sb("ln1_nmr", [P, TILES])
        n1_tm = sb("n1_tm", [P, TOK])
        h_cm = sb("h_cm", [P, TOK])
        h_hi = sb("h_hi", [P, TOK], F32R)
        h_lo = sb("h_lo", [P, TOK], F32R)
        beta_tanh = sb("beta_tanh", [P, TOK])
        beta_cm = sb("beta_cm", [P, TOK])
        vsum_cm = sb("vsum_cm", [P, TOK])
        kv_cm = sb("kv_cm", [P, TOK])
        state_cm = sb("state_cm", [P, 2, TOK])
        o_cm = sb("o_cm", [P, TOK])
        o_hi = sb("o_hi", [P, TOK], F32R)
        o_lo = sb("o_lo", [P, TOK], F32R)
        z_cm = sb("z_cm", [P, TOK])
        xb_tm = sb("xb_tm", [P, 2, TOK])

        lnz_bn = sb("lnz_bn", [P, TILES, 6])
        lnz_mv = sb("lnz_mv", [P, TILES, 2])
        lnz_ve = sb("lnz_ve", [P, TILES])
        lnz_r = sb("lnz_r", [P, TILES])
        nz_tm = sb("nz_tm", [P, TOK])
        nza_tm = sb("nza_tm", [P, TOK])
        x2_tm = sb("x2_tm", [P, 4 * TOK])
        ln2_bn = sb("ln2_bn", [P, TILES, 6])
        ln2_mv = sb("ln2_mv", [P, TILES, 2])
        ln2_ve = sb("ln2_ve", [P, TILES])
        ln2_r = sb("ln2_r", [P, TILES])
        n2_tm = sb("n2_tm", [P, TOK])
        n2c_tm = sb("n2c_tm", [P, TOK])
        h2_tm = sb("h2_tm", [P, TOK])
        ln3_bn = sb("ln3_bn", [P, TILES, 6])
        ln3_mv = sb("ln3_mv", [P, TILES, 2])
        ln3_ve = sb("ln3_ve", [P, TILES])
        ln3_r = sb("ln3_r", [P, TILES])
        scaled_logits = sb("scaled_logits", [P, TILES, E])
        logits = sb("logits", [P, TILES, E])
        top = sb("top", [P, TILES, 8])
        top_ids = sb("top_ids", [P, TILES, 8], U32)
        below = sb("below", [P, TILES, E])
        exp_tanh = sb("exp_tanh", [P, TILES, E])
        exp_den = sb("exp_den", [P, TILES, E])
        exp_rec = sb("exp_rec", [P, TILES, E])
        powers = sb("powers", [P, EXP_SQUARINGS + 1, TILES, E])
        is_first = sb("is_first", [P, TILES, E])
        is_second = sb("is_second", [P, TILES, E])
        chosen = sb("chosen", [P, TILES, E])
        exp_sum = sb("exp_sum", [P, TILES])
        exp_sum_rec = sb("exp_sum_rec", [P, TILES])
        exp_chosen = sb("exp_chosen", [P, TILES, E])
        comb_tm = sb("comb_tm", [P, E, TILES])
        comb_em = sb("comb_em", [E * TILES, P])
        comb_row = sb("comb_row", [1, E * TOK])
        h2_hi = sb("h2_hi", [P, 2, TOK], F32R)
        h2_lo = sb("h2_lo", [P, 2, TOK], F32R)

        comb_cm = sb("comb_cm", [P, 4, TOK])
        gelu_cm = sb("gelu_cm", [P, 2, 2, TOK])
        gelu_hi = sb("gelu_hi", [P, 2, 2, TOK], F32R)
        gelu_lo = sb("gelu_lo", [P, 2, 2, TOK], F32R)
        scaled_cm = sb("scaled_cm", [P, 2, TOK])
        sum_cm = sb("sum_cm", [P, 2, TOK])
        gated_cm = sb("gated_cm", [P, TOK])
        out_tm = sb("out_tm", [P, 2, TOK])

        s_weights = {n: sem("loaded_" + n) for n in
                     ("c", "wmod", "wq", "wk", "wv", "wbeta", "wo", "cols", "gate", "w1", "w2")}
        x_loaded = [sem("x_loaded0"), sem("x_loaded1")]
        row_loaded = sem("row_loaded")
        stored = [sem("stored0"), sem("stored1")]
        ident_zero = sem("ident_zero")
        consts = sem("consts")
        setup_step = sem("setup_step")
        silu_tanh_done = sem("silu_tanh_done")
        silu_done = sem("silu_done")
        mods_ps_done = sem("mods_ps_done")
        mod_cols_done = sem("mod_cols_done")
        half_b_beta_done = sem("half_b_beta_done")
        attn_split = sem("attn_split")
        row_cols_done = sem("row_cols_done")
        gates_done = sem("gates_done")
        gate_gamma_done = sem("gate_gamma_done")
        gate_ps_done = sem("gate_ps_done")
        gate_split = sem("gate_split")
        rows_ps_done = sem("rows_ps_done")
        rows_done = sem("rows_done")
        w1_hi_done = sem("w1_hi_done")
        w2_hi_done = sem("w2_hi_done")
        w1_split = sem("w1_split")
        w2_split = sem("w2_split")
        ln1_bn_done = sem("ln1_bn_done")
        ln1_mv_done = sem("ln1_mv_done")
        ln1_ve_done = sem("ln1_ve_done")
        ln1_r_done = sem("ln1_r_done")
        ln1_neg_done = sem("ln1_neg_done")
        ln1_nmr_done = sem("ln1_nmr_done")
        n1_done = sem("n1_done")
        n1_turned = sem("n1_turned")
        h_done = sem("h_done")
        h_hi_done = sem("h_hi_done")
        h_lo_done = sem("h_lo_done")
        beta_ps_done = sem("beta_ps_done")
        v_ps_done = sem("v_ps_done")
        k_ps_done = sem("k_ps_done")
        q_ps_done = sem("q_ps_done")
        beta_tanh_done = sem("beta_tanh_done")
        vsum_done = sem("vsum_done")
        beta_done = sem("beta_done")
        kv_done = sem("kv_done")
        scan_done = sem("scan_done")
        o_done = sem("o_done")
        o_hi_done = sem("o_hi_done")
        o_lo_done = sem("o_lo_done")
        out_ps_done = sem("out_ps_done")
        z_done = sem("z_done")
        xb_done = sem("xb_done")
        z_turned = sem("z_turned")
        lnz_bn_done = sem("lnz_bn_done")
        lnz_mv_done = sem("lnz_mv_done")
        lnz_ve_done = sem("lnz_ve_done")
        lnz_r_done = sem("lnz_r_done")
        nz_done = sem("nz_done")
        nza_done = sem("nza_done")
        x2_done = sem("x2_done")
        ln2_bn_done = sem("ln2_bn_done")
        ln2_mv_done = sem("ln2_mv_done")
        ln2_ve_done = sem("ln2_ve_done")
        ln2_r_done = sem("ln2_r_done")
        n2_done = sem("n2_done")
        n2c_done = sem("n2c_done")
        h2_done = sem("h2_done")
        ln3_bn_done = sem("ln3_bn_done")
        ln3_mv_done = sem("ln3_mv_done")
        ln3_ve_done = sem("ln3_ve_done")
        ln3_r_done = sem("ln3_r_done")
        logits_ps_done = sem("logits_ps_done")
        logits_scaled = sem("logits_scaled")
        logits_done = sem("logits_done")
        top_done = sem("top_done")
        below_done = sem("below_done")
        exp_tanh_done = sem("exp_tanh_done")
        top_ids_done = sem("top_ids_done")
        den_done = sem("den_done")
        is_top_done = sem("is_top_done")
        rec_done = sem("rec_done")
        chosen_done = sem("chosen_done")
        root_done = sem("root_done")
        squared = sem("squared")
        exp_chosen_done = sem("exp_chosen_done")
        exp_sum_done = sem("exp_sum_done")
        exp_sum_rec_done = sem("exp_sum_rec_done")
        comb_done = sem("comb_done")
        comb_turned = sem("comb_turned")
        comb_em_done = sem("comb_em_done")
        comb_spread = sem("comb_spread")
        h2_turned = sem("h2_turned")
        h2_hi_done = sem("h2_hi_done")
        h2_lo_done = sem("h2_lo_done")
        up_done = sem("up_done")
        gelu_done = sem("gelu_done")
        gelu_hi_done = sem("gelu_hi_done")
        gelu_lo_done = sem("gelu_lo_done")
        down_done = sem("down_done")
        scaled_done = sem("scaled_done")
        sum_done = sem("sum_done")
        gated_done = sem("gated_done")
        gated_turned = sem("gated_turned")
        out_done = sem("out_done")

        block = ctx.enter_context(nc.Block())

        def run(engine, slot):
            def step(experts, late, early):
                for s in range(E):
                    slot(s, experts, late, early)

            step(None, None, Group(0, 0))
            step(None, Group(0, 0), Group(0, 1))
            for k in range(2):
                step(Group(0, k), Group(0, k + 1), Group(0, k + 2))
            with engine.Fori(1, BATCHES - 2) as b:
                for k in range(2):
                    step(Group(b, k), Group(b, k + 1), Group(b, k + 2))
            for k in range(2):
                step(Group(BATCHES - 2, k), Group(BATCHES - 2, k + 1), Group(BATCHES - 2, k + 2))
            last = BATCHES - 1
            step(Group(last, 0), Group(last, 1), None)
            step(Group(last, 1), None, None)

        def tile(t):
            return slice(t * P, (t + 1) * P)

        def tiles_of(rows):
            return lambda t: rows[:, tile(t)]

        CHUNKS = 2 * E
        UP_BANK = [0, 1, 2] * 5 + [1]

        def chunk_before(c):
            for back in range(1, CHUNKS):
                if UP_BANK[(c - back) % CHUNKS] == UP_BANK[c]:
                    return (c - back) % CHUNKS, int(c < back)

        split_before = [sum(e < n for e in SPLIT) for n in range(E + 1)]
        NS = len(SPLIT)

        def first_of_all(g):
            return isinstance(g.b, int) and g.number == 0

        def has_next(g):
            return not (isinstance(g.b, int) and g.number + 1 >= GROUPS)

        def row_of(which, g, tiles=None):
            batch = g.batch
            if tiles is None:
                start = batch * (4 * P) + which * P
                flat = rows[:].rearrange("p b w c -> p (b w c)")
                return flat[:, start:start + P] if isinstance(start, int) else flat[:, bass.ds(start, P)]
            at = slice(batch, batch + 1) if isinstance(batch, int) else bass.ds(batch, 1)
            return rows[:, at, which, :].broadcast_to([P, TILES, P])

        def batch_col(cols_of_batches, g):
            batch = g.batch
            return cols_of_batches[:, batch:batch + 1] if isinstance(batch, int) \
                else cols_of_batches[:, bass.ds(batch, 1)]

        def x2_of(g, first=0, width=TOK):
            start = (g.batch % 2) * (2 * TOK) + (g.slot * TOK + first)
            return x2_tm[:, start:start + width] if isinstance(start, int) else x2_tm[:, bass.ds(start, width)]

        def settle(engine):
            engine.nop(nofuse=True)

        def by_tile(rows):
            return rows.rearrange("p (t c) -> p t c", t=TILES)

        ROW_BANKS = [down_ps[:, 0, :], down_ps[:, 1, :], ps2[:]]

        def gb_of(g):
            return batch_col(gates[:, 1, :], g)

        @block.sync
        def _(sp):
            def load_x(g):
                if exists(g - 2):
                    sp.wait_ge(n1_done, nth(g - 2, 1, 1))
                    settle(sp)
                    sp.wait_ge(xb_done, nth(g - 2, 1, 1))
                settle(sp)
                sp.dma_start(x_tm[:, g.slot, :], x[g.number]).then_inc(x_loaded[g.slot], 16)

            sp.dma_start(c_sb[:], cT).then_inc(s_weights["c"], 16)
            load_x(Group(0, 0))
            sp.dma_start(wmod_sb[:], wmod).then_inc(s_weights["wmod"], 16)
            sp.dma_start(wbeta_sb[:], wbeta).then_inc(s_weights["wbeta"], 16)
            sp.dma_start(wv_sb[:], wv).then_inc(s_weights["wv"], 16)
            sp.dma_start(attn_w[:, K, :], wk).then_inc(s_weights["wk"], 16)
            sp.dma_start(wq_sb[:], wq).then_inc(s_weights["wq"], 16)
            sp.dma_start(attn_w[:, OUT, :], wo).then_inc(s_weights["wo"], 16)
            load_x(Group(0, 1))
            sp.dma_start(w1[:], w1T).then_inc(s_weights["w1"], 16)
            sp.dma_start(w2[:], w2T).then_inc(s_weights["w2"], 16)

            def slot(s, experts, late, early):
                if s == 1 and early and has_next(early) and not first_of_all(early):
                    load_x(early + 1)
                if s == 7 and late:
                    sp.wait_ge(comb_em_done, nth(late, 1, 1))
                    settle(sp)
                    if exists(late - 1):
                        sp.wait_ge(comb_spread, nth(late - 1, E, E))
                        settle(sp)
                    sp.dma_start(comb_row[0:1, :], comb_em[:]).then_inc(row_loaded, 16)
                if s == 7 and experts and exists(experts - 1):
                    store(experts - 1)

            def store(g):
                sp.wait_ge(out_done, nth(g, 1, 1))
                settle(sp)
                sp.dma_start(out[g.number], out_tm[:, g.slot, :]).then_inc(stored[g.slot], 16)

            run(sp, slot)
            store(Group(BATCHES - 1, 1))
            for p in range(2):
                sp.wait_ge(stored[p], 16 * BATCHES)

        @block.gpsimd
        def _(pool):
            nc.gpsimd.memset(ident[:], 0.0).then_inc(ident_zero, 1)
            pool.wait_ge(ident_zero, 1)
            nc.gpsimd.affine_select(out=ident[:], in_=ident[:], compare_op=ALU.not_equal, fill=1.0, base=0,
                                    pattern=[[-1, P]], channel_multiplier=1).then_inc(consts, 1)
            nc.gpsimd.memset(minus_half[:], -0.5).then_inc(consts, 1)
            nc.gpsimd.iota(expert_ids[:], pattern=[[0, TILES], [1, E]], base=0, channel_multiplier=0,
                           allow_small_or_imprecise_dtypes=True).then_inc(consts, 1)
            nc.gpsimd.memset(mean_w[:], 1.0 / P).then_inc(consts, 1)
            pool.wait_ge(consts, 4)

            def rstd(g, mv, mv_done, ve, ve_done, r, r_done, r_used):
                pool.wait_ge(mv_done, nth(g, 1, 1))
                settle(pool)
                nc.gpsimd.tensor_scalar(ve[:], mv[:, :, 1], 1.0, EPS, ALU.mult, ALU.add).then_inc(ve_done, 1)
                pool.wait_ge(ve_done, nth(g, 1, 1))
                if exists(g - 1):
                    pool.wait_ge(r_used, nth(g - 1, 1, 1))
                nc.gpsimd.tensor_tensor(r[:], ve[:], minus_half[:], ALU.pow).then_inc(r_done, 1)

            def ln1_scales(g):
                rstd(g, ln1_mv, ln1_mv_done, ln1_ve, ln1_ve_done, ln1_r, ln1_r_done, n1_done)
                nc.gpsimd.tensor_scalar(ln1_neg[:], ln1_mv[:, :, 0], -1.0, 0.0, ALU.mult, ALU.add)\
                    .then_inc(ln1_neg_done, 1)
                pool.wait_ge(ln1_neg_done, nth(g, 1, 1))
                settle(pool)
                pool.wait_ge(ln1_r_done, nth(g, 1, 1))
                nc.gpsimd.tensor_tensor(ln1_nmr[:], ln1_neg[:], ln1_r[:], ALU.mult).then_inc(ln1_nmr_done, 1)

            def spread(g, e):
                if e == 0:
                    pool.wait_ge(row_loaded, nth(g, 16, 16))
                if e >= 4:
                    pool.wait_ge(scaled_done, nth(g, E, e - 3))
                elif exists(g - 1):
                    pool.wait_ge(scaled_done, nth(g - 1, E, e + 5))
                settle(pool)
                nc.gpsimd.partition_broadcast(comb_cm[:, e % 4, :], comb_row[0:1, e * TOK:(e + 1) * TOK], P)\
                    .then_inc(comb_spread, 1)

            def add_expert(g, e):
                pool.wait_ge(scaled_done, nth(g, E, e + 1))
                if e >= 2:
                    pool.wait_ge(sum_done, nth(g, E - 1, e - 1))
                nc.gpsimd.tensor_tensor(sum_cm[:, g.slot, :], sum_cm[:, g.slot, :], scaled_cm[:, e % 2, :], ALU.add)\
                    .then_inc(sum_done, 1)

            def slot(s, experts, late, early):
                if experts and s == 0 and exists(experts - 1):
                    add_expert(experts - 1, E - 1)
                if late:
                    if s == 0:
                        rstd(late, lnz_mv, lnz_mv_done, lnz_ve, lnz_ve_done, lnz_r, lnz_r_done, nz_done)
                    if s == 2:
                        rstd(late, ln2_mv, ln2_mv_done, ln2_ve, ln2_ve_done, ln2_r, ln2_r_done, n2_done)
                if early and s == 1:
                    pool.wait_ge(h_hi_done, nth(early, 1, 1))
                    if exists(early - 1):
                        pool.wait_ge(q_ps_done, nth(early - 1, 1, 1))
                    nc.gpsimd.tensor_tensor(h_lo[:], h_cm[:], h_hi[:].bitcast(F32), ALU.subtract)\
                        .then_inc(h_lo_done, 1)
                if experts:
                    if s == 0:
                        spread(experts, 0)
                    elif s == 1:
                        spread(experts, 1)
                        spread(experts, 2)
                    elif s < 7:
                        spread(experts, s + 1)
                    if s >= 2:
                        add_expert(experts, s - 1)
                if late and s == 4:
                    rstd(late, ln3_mv, ln3_mv_done, ln3_ve, ln3_ve_done, ln3_r, ln3_r_done, logits_scaled)
                if early:
                    if s == 5:
                        if first_of_all(early):
                            pool.wait_ge(rows_done, BATCHES)
                        if exists(early - 2):
                            pool.wait_ge(x2_done, nth(early - 2, 1, 1))
                        settle(pool)
                        nc.gpsimd.tensor_tensor(by_tile(xb_tm[:, early.slot, :]), by_tile(x_tm[:, early.slot, :]),
                                                row_of(SHIFT_A, early, TILES), ALU.add).then_inc(xb_done, 1)
                    if s == 6 and has_next(early):
                        ln1_scales(early + 1)

            ln1_scales(Group(0, 0))
            run(pool, slot)
            add_expert(Group(BATCHES - 1, 1), E - 1)

        @block.scalar
        def _(act):
            for n, row in enumerate((b_o, gamma, beta_, ln_g, ln_b)):
                act.dma_start(cols[:, n + 1:n + 2], row.rearrange("(c o) -> c o", o=1)).then_inc(s_weights["cols"], 16)
            act.dma_start(cols[:, 0:1], b_beta.rearrange("(h o) -> h o", o=1).broadcast_to([HEADS, D]))\
                .then_inc(s_weights["cols"], 16)
            act.dma_start(gate[:], gateT).then_inc(s_weights["gate"], 16)
            act.wait_ge(s_weights["c"], 16)
            nc.scalar.activation(c_tanh[:], c_sb[:], ACT.Tanh, scale=0.5).then_inc(silu_tanh_done, 1)

            def first_norm(g):
                act.wait_ge(ln1_nmr_done, nth(g, 1, 1))
                if exists(g - 1):
                    act.wait_ge(n1_turned, nth(g - 1, 1, 1))
                for t in range(TILES):
                    ins = nc.scalar.activation(n1_tm[:, tile(t)], x_tm[:, g.slot, tile(t)], ACT.Identity,
                                               scale=ln1_r[:, t:t + 1], bias=ln1_nmr[:, t:t + 1])
                ins.then_inc(n1_done, 1)

            def gelu(g, e):
                for f in range(2):
                    c = 2 * e + f
                    act.wait_ge(up_done, nth(g, CHUNKS, c + 1))
                    if f == 0:
                        if e >= 2:
                            act.wait_ge(down_done, nth(g, E, e - 1))
                        elif exists(g - 1):
                            act.wait_ge(down_done, nth(g - 1, E, e + 7))
                    if e in SPLIT:
                        nc.scalar.activation(gelu_hi[:, e % 2, f, :], up_ps[:, UP_BANK[c], :], ACT.Gelu)\
                            .then_inc(gelu_hi_done, 1)
                    nc.scalar.activation(gelu_cm[:, e % 2, f, :], up_ps[:, UP_BANK[c], :], ACT.Gelu)\
                        .then_inc(gelu_done, 1)

            def gate_sum(g):
                act.wait_ge(sum_done, nth(g, E - 1, E - 1))
                if exists(g - 1):
                    act.wait_ge(gated_turned, nth(g - 1, 1, 1))
                settle(act)
                nc.scalar.activation(gated_cm[:], sum_cm[:, g.slot, :], ACT.Copy, scale=gb_of(g))\
                    .then_inc(gated_done, 1)

            def slot(s, experts, late, early):
                if s == 7 and late:
                    act.wait_ge(root_done, nth(late, 1, 1))
                    for n in range(EXP_SQUARINGS):
                        if n:
                            act.wait_ge(squared, nth(late, EXP_SQUARINGS, n))
                        elif exists(late - 1):
                            act.wait_ge(exp_sum_done, nth(late - 1, 1, 1))
                        nc.scalar.activation(powers[:, n + 1], powers[:, n], ACT.Square).then_inc(squared, 1)
                if experts and s < 7:
                    gelu(experts, s + 1)
                if s == 7 and late:
                    gelu(late, 0)
                if early and s == 7 and has_next(early):
                    first_norm(early + 1)
                if s == 5 and experts and exists(experts - 1):
                    gate_sum(experts - 1)
                if early:
                    if s == 0:
                        act.wait_ge(n1_turned, nth(early, 1, 1))
                        if first_of_all(early):
                            act.wait_ge(mod_cols_done, 1)
                        if exists(early - 1):
                            act.wait_ge(z_done, nth(early - 1, 1, 1))
                        settle(act)
                        nc.scalar.activation(h_cm[:], ps1[:], ACT.Identity, scale=batch_col(scale_h[:], early),
                                             bias=batch_col(mods[:, 0, :], early)).then_inc(h_done, 1)
                        act.wait_ge(h_done, nth(early, 1, 1))
                        if exists(early - 1):
                            act.wait_ge(q_ps_done, nth(early - 1, 1, 1))
                        nc.scalar.activation(h_hi[:], h_cm[:], ACT.Copy).then_inc(h_hi_done, 1)
                    if s == 2:
                        act.wait_ge(beta_ps_done, nth(early, 1, 1))
                        if first_of_all(early):
                            act.wait_ge(half_b_beta_done, 1)
                        if exists(early - 1):
                            act.wait_ge(beta_done, nth(early - 1, 1, 1))
                        nc.scalar.activation(beta_tanh[:], ps1[:], ACT.Tanh, scale=0.5, bias=half_b_beta[:])\
                            .then_inc(beta_tanh_done, 1)
                        act.wait_ge(v_ps_done, nth(early, 1, 1))
                        if exists(early - 1):
                            act.wait_ge(kv_done, nth(early - 1, 1, 1))
                        nc.scalar.activation(vsum_cm[:], ps0[:], ACT.Copy).then_inc(vsum_done, 1)
                        if first_of_all(early):
                            for b in range(BATCHES):
                                act.wait_ge(rows_ps_done, b + 1)
                                nc.scalar.activation(rows[:, b].rearrange("p w c -> p (w c)"), ROW_BANKS[b % 3],
                                                     ACT.Copy).then_inc(rows_done, 1)
                    if s == 5:
                        act.wait_ge(o_done, nth(early, 1, 1))
                        if exists(early - 1):
                            act.wait_ge(out_ps_done, nth(early - 1, 1, 1))
                        nc.scalar.activation(o_hi[:], o_cm[:], ACT.Copy).then_inc(o_hi_done, 1)
                        if first_of_all(early):
                            act.wait_ge(s_weights["w1"], 16)
                            nc.scalar.activation(w1_hi[:], w1[:], ACT.Copy).then_inc(w1_hi_done, 1)
                            act.wait_ge(s_weights["w2"], 16)
                            nc.scalar.activation(w2_hi[:], w2[:], ACT.Copy).then_inc(w2_hi_done, 1)
                if late:
                    if s == 4:
                        act.wait_ge(h2_turned, nth(late, 1, 1))
                        if exists(late - 2):
                            act.wait_ge(up_done, nth(late - 2, CHUNKS, CHUNKS))
                        nc.scalar.activation(h2_hi[:, late.slot, :], ps2[:], ACT.Copy).then_inc(h2_hi_done, 1)
                    if s == 6:
                        act.wait_ge(below_done, nth(late, 1, 1))
                        if exists(late - 1):
                            act.wait_ge(root_done, nth(late - 1, 1, 1))
                        nc.scalar.activation(exp_tanh[:], below[:], ACT.Tanh, scale=0.5 / 2 ** EXP_SQUARINGS)\
                            .then_inc(exp_tanh_done, 1)
                    if s == 7:
                        act.wait_ge(comb_turned, nth(late, 1, 1))
                        if exists(late - 1):
                            act.wait_ge(row_loaded, nth(late - 1, 16, 16))
                        nc.scalar.activation(comb_em[:], ps2[0:E * TILES, 0:P], ACT.Copy).then_inc(comb_em_done, 1)

            first_norm(Group(0, 0))
            run(act, slot)
            gate_sum(Group(BATCHES - 1, 1))

        @block.vector
        def _(dve):
            done = [0]

            def then(ins):
                done[0] += 1
                ins.then_inc(setup_step, 1)
                dve.wait_ge(setup_step, done[0])

            def first_stats(g):
                dve.wait_ge(x_loaded[g.slot], turn(g))
                stats(g, tiles_of(x_tm[:, g.slot, :]), ln1_bn, ln1_bn_done, ln1_mv, ln1_mv_done, ln1_nmr_done)

            def stats(g, src, bn, bn_done, mv, mv_done, mv_used):
                settle(dve)
                for t in range(TILES):
                    ins = nc.vector.bn_stats(bn[:, t, :], src(t))
                ins.then_inc(bn_done, 1)
                dve.wait_ge(bn_done, nth(g, 1, 1))
                if exists(g - 1):
                    dve.wait_ge(mv_used, nth(g - 1, 1, 1))
                settle(dve)
                for t in range(TILES):
                    ins = nc.vector.bn_aggr(mv[:, t, :], bn[:, t, :])
                ins.then_inc(mv_done, 1)

            dve.wait_ge(silu_tanh_done, 1)
            then(nc.vector.tensor_scalar(c_sig[:], c_tanh[:], 0.5, 0.5, ALU.mult, ALU.add))
            nc.vector.tensor_tensor(silu_c[:], c_sb[:], c_sig[:], ALU.mult).then_inc(silu_done, 1)
            first_stats(Group(0, 0))
            dve.wait_ge(s_weights["cols"], 96)
            nc.vector.tensor_scalar(half_b_beta[:], cols[:, 0:1], 0.5, None, ALU.mult).then_inc(half_b_beta_done, 1)

            def by_head(row):
                return row.rearrange("p (h d) -> p h d", h=HEADS)

            def repeated(row):
                return row.rearrange("p (h o) -> p h o", o=1).broadcast_to([P, HEADS, D])

            dve.wait_ge(s_weights["wbeta"], 16)
            nc.vector.tensor_copy(by_head(attn_w[:, BETA, :]), repeated(wbeta_sb[:]))
            dve.wait_ge(s_weights["wv"], 16)
            nc.vector.tensor_reduce(head_sums[:, 0, :], by_head(wv_sb[:]), AX_X, ALU.add)
            dve.wait_ge(mods_ps_done, 1)
            then(nc.vector.tensor_copy(mods[:].rearrange("p j b -> p (j b)"), ps0[:, 0:6 * BATCHES]))
            nc.vector.tensor_scalar(scale_h[:], mods[:, 1, :], 1.0, None, ALU.add).then_inc(mod_cols_done, 1)
            dve.wait_ge(s_weights["wq"], 16)
            then(nc.vector.tensor_reduce(head_sums[:, 1, :], by_head(wq_sb[:]), AX_X, ALU.add))
            nc.vector.tensor_copy(by_head(attn_w[:, V, :]), repeated(head_sums[:, 0, :]))
            then(nc.vector.tensor_copy(by_head(attn_w[:, Q, :]), repeated(head_sums[:, 1, :])))
            dve.wait_ge(s_weights["wk"], 16)
            dve.wait_ge(s_weights["wo"], 16)
            then(nc.vector.tensor_copy(attn_hi[:], attn_w[:]))
            nc.vector.tensor_tensor(attn_lo[:], attn_w[:], attn_hi[:].bitcast(F32), ALU.subtract)\
                .then_inc(attn_split, 1)
            gagb = mods[:].rearrange("p (h j) b -> p h j b", j=3)[:, :, 2, :]
            then(nc.vector.tensor_scalar(sign[:], gagb, 0.0, 2.0, ALU.is_ge, ALU.mult))
            then(nc.vector.tensor_scalar(sign[:], sign[:], -1.0, None, ALU.add))
            then(nc.vector.tensor_tensor(size[:], gagb, sign[:], ALU.mult))
            nc.vector.scalar_tensor_tensor(out=gates[:], in0=size[:], scalar=GATE_FLOOR, in1=sign[:],
                                           op0=ALU.max, op1=ALU.mult).then_inc(gates_done, 1)
            nc.vector.tensor_scalar(row_cols[:, :, SCALE_B], mods[:, 4, :], 1.0, None, ALU.add)
            nc.vector.tensor_copy(row_cols[:, :, SHIFT_B], mods[:, 3, :])
            dve.wait_ge(gates_done, 1)
            nc.vector.tensor_scalar(row_cols[:, :, SCALE_A], gates[:, 0, :], cols[:, 4:5], None, ALU.mult)
            nc.vector.tensor_scalar(row_cols[:, :, SHIFT_A], gates[:, 0, :], cols[:, 5:6], None, ALU.mult)\
                .then_inc(row_cols_done, 1)
            dve.wait_ge(s_weights["gate"], 16)
            nc.vector.tensor_scalar(gate_gamma[:], gate[:], cols[:, 2:3], None, ALU.mult).then_inc(gate_gamma_done, 1)
            dve.wait_ge(consts, 4)

            def normalize(dst, src, mv, r, n_done):
                for t in range(TILES):
                    ins = nc.vector.tensor_scalar(dst[:, tile(t)], src(t), mv[:, t, 0:1], r[:, t:t + 1],
                                                  ALU.subtract, ALU.mult)
                ins.then_inc(n_done, 1)

            def scale_expert(g, e):
                dve.wait_ge(down_done, nth(g, E, e + 1))
                dve.wait_ge(comb_spread, nth(g, E, e + 1))
                if e == 0:
                    if exists(g - 2):
                        dve.wait_ge(gated_done, nth(g - 2, 1, 1))
                    dst = sum_cm[:, g.slot, :]
                else:
                    if e >= 3:
                        dve.wait_ge(sum_done, nth(g, E - 1, e - 2))
                    elif exists(g - 1):
                        dve.wait_ge(sum_done, nth(g - 1, E - 1, 6 if e == 2 else 7))
                    dst = scaled_cm[:, e % 2, :]
                nc.vector.tensor_tensor(dst, down_ps[:, e % 2, :], comb_cm[:, e % 4, :], ALU.mult)\
                    .then_inc(scaled_done, 1)

            def gelu_low(g, e):
                dve.wait_ge(gelu_done, nth(g, CHUNKS, 2 * e + 2))
                dve.wait_ge(gelu_hi_done, nth(g, 2 * NS, 2 * split_before[e] + 2))
                nc.vector.tensor_tensor(gelu_lo[:, e % 2], gelu_cm[:, e % 2], gelu_hi[:, e % 2].bitcast(F32),
                                        ALU.subtract).then_inc(gelu_lo_done, 1)

            def add_residual(g):
                dve.wait_ge(gated_turned, nth(g, 1, 1))
                if exists(g - 2):
                    dve.wait_ge(stored[g.slot], turn(g - 2))
                nc.vector.tensor_tensor(out_tm[:, g.slot, :], ps0[:], x2_of(g), ALU.add)\
                    .then_inc(out_done, 1)

            def early_work(s, early):
                if s == 4:
                    dve.wait_ge(beta_tanh_done, nth(early, 1, 1))
                    if exists(early - 1):
                        dve.wait_ge(scan_done, nth(early - 1, 1, 1))
                    nc.vector.tensor_scalar(beta_cm[:], beta_tanh[:], 0.5, 0.5, ALU.mult, ALU.add)\
                        .then_inc(beta_done, 1)
                    dve.wait_ge(k_ps_done, nth(early, 1, 1))
                    dve.wait_ge(vsum_done, nth(early, 1, 1))
                    nc.vector.tensor_tensor(kv_cm[:], ps1[:], vsum_cm[:], ALU.mult).then_inc(kv_done, 1)
                    dve.wait_ge(beta_done, nth(early, 1, 1))
                    dve.wait_ge(kv_done, nth(early, 1, 1))
                    if exists(early - 2):
                        dve.wait_ge(o_done, nth(early - 2, 1, 1))
                    start = 0.0 if early.slot == 0 else state_cm[:, 0, TOK - 1:TOK]
                    nc.vector.tensor_tensor_scan(state_cm[:, early.slot, :], beta_cm[:], kv_cm[:], start,
                                                 ALU.mult, ALU.add).then_inc(scan_done, 1)
                    dve.wait_ge(scan_done, nth(early, 1, 1))
                    dve.wait_ge(q_ps_done, nth(early, 1, 1))
                    if exists(early - 1):
                        dve.wait_ge(o_lo_done, nth(early - 1, 1, 1))
                    nc.vector.tensor_tensor(o_cm[:], ps0[:], state_cm[:, early.slot, :], ALU.mult)\
                        .then_inc(o_done, 1)
                if s == 5:
                    dve.wait_ge(o_hi_done, nth(early, 1, 1))
                    nc.vector.tensor_tensor(o_lo[:], o_cm[:], o_hi[:].bitcast(F32), ALU.subtract)\
                        .then_inc(o_lo_done, 1)
                    if first_of_all(early):
                        dve.wait_ge(w1_hi_done, 1)
                        nc.vector.tensor_tensor(w1_lo[:], w1[:], w1_hi[:].bitcast(F32), ALU.subtract)\
                            .then_inc(w1_split, 1)
                        dve.wait_ge(w2_hi_done, 1)
                        nc.vector.tensor_tensor(w2_lo[:], w2[:], w2_hi[:].bitcast(F32), ALU.subtract)\
                            .then_inc(w2_split, 1)
                        dve.wait_ge(gate_ps_done, 1)
                        then(nc.vector.tensor_tensor(gate_mid[:], gate_gamma[:], ps2[:, 0:E], ALU.subtract))
                        nc.vector.tensor_copy(gate_bias[:], ps2[:, E:2 * E])
                        then(nc.vector.tensor_copy(gate_hi[:], gate_mid[:]))
                        nc.vector.tensor_tensor(gate_lo[:], gate_mid[:], gate_hi[:].bitcast(F32), ALU.subtract)\
                            .then_inc(gate_split, 1)
                if s == 7:
                    dve.wait_ge(out_ps_done, nth(early, 1, 1))
                    if exists(early - 1):
                        dve.wait_ge(z_turned, nth(early - 1, 1, 1))
                    nc.vector.scalar_tensor_tensor(out=z_cm[:], in0=ps1[:], scalar=cols[:, 1:2], in1=h_cm[:],
                                                   op0=ALU.add, op1=ALU.add).then_inc(z_done, 1)

            def late_work(s, late):
                if s == 0:
                    dve.wait_ge(z_turned, nth(late, 1, 1))
                    stats(late, tiles_of(ps0), lnz_bn, lnz_bn_done, lnz_mv, lnz_mv_done, nz_done)
                if s == 1:
                    dve.wait_ge(lnz_r_done, nth(late, 1, 1))
                    normalize(nz_tm, tiles_of(ps0), lnz_mv, lnz_r, nz_done)
                    dve.wait_ge(nz_done, nth(late, 1, 1))
                    if not exists(late - 1):
                        dve.wait_ge(rows_done, BATCHES)
                    nc.vector.tensor_tensor(by_tile(nza_tm[:]), by_tile(nz_tm[:]), row_of(SCALE_A, late, TILES),
                                            ALU.mult).then_inc(nza_done, 1)
                    dve.wait_ge(nza_done, nth(late, 1, 1))
                    dve.wait_ge(xb_done, nth(late, 1, 1))
                    nc.vector.tensor_tensor(x2_of(late), nza_tm[:], xb_tm[:, late.slot, :], ALU.add)\
                        .then_inc(x2_done, 1)
                if s == 2:
                    dve.wait_ge(x2_done, nth(late, 1, 1))
                    stats(late, lambda t: x2_of(late, t * P, P), ln2_bn, ln2_bn_done, ln2_mv, ln2_mv_done, n2_done)
                if s == 3:
                    dve.wait_ge(ln2_r_done, nth(late, 1, 1))
                    normalize(n2_tm, lambda t: x2_of(late, t * P, P), ln2_mv, ln2_r, n2_done)
                    dve.wait_ge(n2_done, nth(late, 1, 1))
                    nc.vector.tensor_tensor(by_tile(n2c_tm[:]), by_tile(n2_tm[:]), row_of(SCALE_B, late, TILES),
                                            ALU.mult).then_inc(n2c_done, 1)
                    dve.wait_ge(n2c_done, nth(late, 1, 1))
                    if exists(late - 1):
                        dve.wait_ge(h2_turned, nth(late - 1, 1, 1))
                    nc.vector.tensor_tensor(by_tile(h2_tm[:]), by_tile(n2c_tm[:]), row_of(SHIFT_B, late, TILES),
                                            ALU.add).then_inc(h2_done, 1)
                    dve.wait_ge(h2_done, nth(late, 1, 1))
                    stats(late, tiles_of(h2_tm), ln3_bn, ln3_bn_done, ln3_mv, ln3_mv_done, ln3_ve_done)
                if s == 6:
                    dve.wait_ge(logits_ps_done, nth(late, 1, 1))
                    dve.wait_ge(ln3_r_done, nth(late, 1, 1))
                    nc.vector.tensor_tensor(scaled_logits[:], ps2[:, 0:TILES * E].rearrange("p (t e) -> p t e", e=E),
                                            ln3_r[:].rearrange("p (t o) -> p t o", o=1).broadcast_to([P, TILES, E]),
                                            ALU.mult).then_inc(logits_scaled, 1)
                    dve.wait_ge(logits_scaled, nth(late, 1, 1))
                    nc.vector.tensor_tensor(logits[:], scaled_logits[:],
                                            gate_bias[:].rearrange("p (o e) -> p o e", o=1)
                                            .broadcast_to([P, TILES, E]), ALU.add).then_inc(logits_done, 1)
                    dve.wait_ge(logits_done, nth(late, 1, 1))
                    settle(dve)
                    for t in range(TILES):
                        ins = nc.vector.max(top[:, t, :], logits[:, t, :])
                    ins.then_inc(top_done, 1)
                    dve.wait_ge(top_done, nth(late, 1, 1))
                    nc.vector.tensor_tensor(below[:], logits[:], top[:, :, 0:1].broadcast_to([P, TILES, E]),
                                            ALU.subtract).then_inc(below_done, 1)
                    for t in range(TILES):
                        ins = nc.vector.max_index(top_ids[:, t, :], top[:, t, :], logits[:, t, :])
                    ins.then_inc(top_ids_done, 1)
                    dve.wait_ge(top_ids_done, nth(late, 1, 1))
                    nc.vector.tensor_tensor(is_first[:], expert_ids[:], top_ids[:, :, 0:1].broadcast_to([P, TILES, E]),
                                            ALU.is_equal)
                    nc.vector.tensor_tensor(is_second[:], expert_ids[:], top_ids[:, :, 1:2].broadcast_to([P, TILES, E]),
                                            ALU.is_equal).then_inc(is_top_done, 1)
                    dve.wait_ge(exp_tanh_done, nth(late, 1, 1))
                    nc.vector.tensor_scalar(exp_den[:], exp_tanh[:], -1.0, 1.0, ALU.mult, ALU.add).then_inc(den_done, 1)
                    dve.wait_ge(is_top_done, nth(late, 1, 1))
                    nc.vector.tensor_tensor(chosen[:], is_first[:], is_second[:], ALU.add).then_inc(chosen_done, 1)
                    dve.wait_ge(den_done, nth(late, 1, 1))
                    nc.vector.reciprocal(exp_rec[:], exp_den[:]).then_inc(rec_done, 1)
                    dve.wait_ge(rec_done, nth(late, 1, 1))
                    if exists(late - 1):
                        dve.wait_ge(squared, nth(late - 1, EXP_SQUARINGS, 1))
                    nc.vector.scalar_tensor_tensor(out=powers[:, 0], in0=exp_tanh[:], scalar=1.0, in1=exp_rec[:],
                                                   op0=ALU.add, op1=ALU.mult).then_inc(root_done, 1)
                if s == 7:
                    dve.wait_ge(squared, nth(late, EXP_SQUARINGS, EXP_SQUARINGS))
                    dve.wait_ge(chosen_done, nth(late, 1, 1))
                    nc.vector.tensor_reduce(exp_sum[:], powers[:, EXP_SQUARINGS], AX_X, ALU.add)\
                        .then_inc(exp_sum_done, 1)
                    nc.vector.tensor_tensor(exp_chosen[:], powers[:, EXP_SQUARINGS], chosen[:], ALU.mult)\
                        .then_inc(exp_chosen_done, 1)
                    dve.wait_ge(exp_sum_done, nth(late, 1, 1))
                    nc.vector.reciprocal(exp_sum_rec[:], exp_sum[:]).then_inc(exp_sum_rec_done, 1)
                    dve.wait_ge(exp_sum_rec_done, nth(late, 1, 1))
                    dve.wait_ge(exp_chosen_done, nth(late, 1, 1))
                    if exists(late - 1):
                        dve.wait_ge(comb_turned, nth(late - 1, 1, 1))
                    nc.vector.tensor_tensor(comb_tm[:].rearrange("p e t -> p t e"), exp_chosen[:],
                                            exp_sum_rec[:].rearrange("p (t o) -> p t o", o=1)
                                            .broadcast_to([P, TILES, E]), ALU.mult).then_inc(comb_done, 1)

            def slot(s, experts, late, early):
                if s == 5 and late:
                    dve.wait_ge(h2_hi_done, nth(late, 1, 1))
                    nc.vector.tensor_tensor(h2_lo[:, late.slot, :], ps2[:], h2_hi[:, late.slot, :].bitcast(F32),
                                            ALU.subtract).then_inc(h2_lo_done, 1)
                if experts:
                    if s:
                        scale_expert(experts, s - 1)
                    elif exists(experts - 1):
                        scale_expert(experts - 1, E - 1)
                if early and s == 6 and has_next(early):
                    first_stats(early + 1)
                if late:
                    late_work(s, late)
                if s == 7 and experts and exists(experts - 1):
                    add_residual(experts - 1)
                if early:
                    early_work(s, early)
                if experts and s < 7 and s + 1 in SPLIT:
                    gelu_low(experts, s + 1)
                if late and s == 7 and 0 in SPLIT:
                    gelu_low(late, 0)

            run(dve, slot)
            scale_expert(Group(BATCHES - 1, 1), E - 1)
            add_residual(Group(BATCHES - 1, 1))

        @block.tensor
        def _(pe):
            pe.wait_ge(s_weights["wmod"], 16)
            pe.wait_ge(silu_done, 1)
            for n in range(6):
                ins = nc.tensor.matmul(ps0[:, n * BATCHES:(n + 1) * BATCHES], wmod_sb[:, n * P:(n + 1) * P], silu_c[:],
                                       start=True, stop=True)
            ins.then_inc(mods_ps_done, 1)

            def product(dst, w_hi, w_lo, x_hi, x_lo):
                nc.tensor.matmul(dst, w_hi, x_hi, start=True, stop=False)
                nc.tensor.matmul(dst, w_lo, x_hi, start=False, stop=False)
                return nc.tensor.matmul(dst, w_hi, x_lo, start=False, stop=True)

            def turn_tiles(dst, src):
                for t in range(TILES):
                    ins = nc.tensor.transpose(dst[:, tile(t)], src[:, tile(t)], ident[:])
                return ins

            def project(dst, which, x_hi, x_lo):
                return product(dst, attn_hi[:, which, :], attn_lo[:, which, :], x_hi[:], x_lo[:])

            def up(g, e):
                if e == 0:
                    pe.wait_ge(h2_hi_done, nth(g, 1, 1))
                    pe.wait_ge(h2_lo_done, nth(g, 1, 1))
                for f in range(2):
                    c = 2 * e + f
                    before, back = chunk_before(c)
                    if exists(g - back):
                        pe.wait_ge(gelu_done, nth(g - back, CHUNKS, before + 1))
                    w = slice(c * P, (c + 1) * P)
                    product(up_ps[:, UP_BANK[c], :], w1_hi[:, w], w1_lo[:, w],
                            h2_hi[:, g.slot, :], h2_lo[:, g.slot, :]).then_inc(up_done, 1)

            def down(g, e):
                if e >= 2:
                    pe.wait_ge(scaled_done, nth(g, E, e - 1))
                elif exists(g - 1):
                    pe.wait_ge(scaled_done, nth(g - 1, E, e + 7))
                dst = down_ps[:, e % 2, :]
                if e in SPLIT:
                    for f in range(2):
                        pe.wait_ge(gelu_hi_done, nth(g, 2 * NS, 2 * split_before[e] + f + 1))
                        nc.tensor.matmul(dst, w2_hi[:, e, f, :], gelu_hi[:, e % 2, f, :], start=f == 0, stop=False)
                        nc.tensor.matmul(dst, w2_lo[:, e, f, :], gelu_hi[:, e % 2, f, :], start=False, stop=False)
                    pe.wait_ge(gelu_lo_done, nth(g, NS, split_before[e] + 1))
                    for f in range(2):
                        ins = nc.tensor.matmul(dst, w2_hi[:, e, f, :], gelu_lo[:, e % 2, f, :], start=False,
                                               stop=f == 1)
                else:
                    for f in range(2):
                        pe.wait_ge(gelu_done, nth(g, CHUNKS, 2 * e + f + 1))
                        ins = nc.tensor.matmul(dst, w2[:, e, f, :], gelu_cm[:, e % 2, f, :], start=f == 0, stop=f == 1)
                ins.then_inc(down_done, 1)

            def turn_gated(g):
                pe.wait_ge(gated_done, nth(g, 1, 1))
                turn_tiles(ps0, gated_cm).then_inc(gated_turned, 1)

            def make_rows():
                pe.wait_ge(row_cols_done, 1)
                for b in range(BATCHES):
                    if b >= 3:
                        pe.wait_ge(rows_done, b - 2)
                    for j in range(4):
                        ins = nc.tensor.matmul(ROW_BANKS[b % 3][:, j * P:(j + 1) * P],
                                               row_cols[:, b, j:j + 1].broadcast_to([P, P]), ident[:],
                                               start=True, stop=True)
                    ins.then_inc(rows_ps_done, 1)

            def slot(s, experts, late, early):
                if s == 6 and late:
                    if not exists(late - 1):
                        pe.wait_ge(gate_split, 1)
                    pe.wait_ge(h2_lo_done, nth(late, 1, 1))
                    for t in range(TILES):
                        hi, lo = h2_hi[:, late.slot, tile(t)], h2_lo[:, late.slot, tile(t)]
                        ins = product(ps2[:, t * E:(t + 1) * E], hi, lo, gate_hi[:], gate_lo[:])
                    ins.then_inc(logits_ps_done, 1)
                if experts and s < 7:
                    up(experts, s + 1)
                if s == 7 and late:
                    if not exists(late - 1):
                        pe.wait_ge(w1_split, 1)
                    up(late, 0)
                if s == 0 and late:
                    pe.wait_ge(z_done, nth(late, 1, 1))
                    turn_tiles(ps0, z_cm).then_inc(z_turned, 1)
                if s == 0 and early:
                    pe.wait_ge(n1_done, nth(early, 1, 1))
                    if not exists(early - 1):
                        pe.wait_ge(consts, 4)
                    turn_tiles(ps1, n1_tm).then_inc(n1_turned, 1)
                if s == 2 and early:
                    if not exists(early - 1):
                        pe.wait_ge(attn_split, 1)
                    pe.wait_ge(h_hi_done, nth(early, 1, 1))
                    pe.wait_ge(h_lo_done, nth(early, 1, 1))
                    project(ps1[:], BETA, h_hi, h_lo).then_inc(beta_ps_done, 1)
                    if late:
                        pe.wait_ge(nz_done, nth(late, 1, 1))
                    project(ps0[:], V, h_hi, h_lo).then_inc(v_ps_done, 1)
                if s == 3 and early:
                    pe.wait_ge(beta_tanh_done, nth(early, 1, 1))
                    project(ps1[:], K, h_hi, h_lo).then_inc(k_ps_done, 1)
                    pe.wait_ge(vsum_done, nth(early, 1, 1))
                    project(ps0[:], Q, h_hi, h_lo).then_inc(q_ps_done, 1)
                    if first_of_all(early):
                        make_rows()
                        pe.wait_ge(rows_done, BATCHES)
                        pe.wait_ge(gate_gamma_done, 1)
                        nc.tensor.matmul(ps2[:, 0:E], mean_w[:], gate_gamma[:], start=True, stop=True)
                        nc.tensor.matmul(ps2[:, E:2 * E], cols[:, 3:4].broadcast_to([P, P]), gate[:],
                                         start=True, stop=True).then_inc(gate_ps_done, 1)
                if s == 4 and late:
                    pe.wait_ge(h2_done, nth(late, 1, 1))
                    if exists(late - 1):
                        pe.wait_ge(comb_em_done, nth(late - 1, 1, 1))
                    else:
                        pe.wait_ge(gate_split, 1)
                    turn_tiles(ps2, h2_tm).then_inc(h2_turned, 1)
                if s == 6:
                    if experts and exists(experts - 1):
                        if early:
                            pe.wait_ge(o_done, nth(early, 1, 1))
                        turn_gated(experts - 1)
                    if early:
                        pe.wait_ge(o_hi_done, nth(early, 1, 1))
                        pe.wait_ge(o_lo_done, nth(early, 1, 1))
                        pe.wait_ge(kv_done, nth(early, 1, 1))
                        project(ps1[:], OUT, o_hi, o_lo).then_inc(out_ps_done, 1)
                if experts:
                    if s == 0 and not exists(experts - 1):
                        pe.wait_ge(w2_split, 1)
                    down(experts, s)
                if s == 7 and late:
                    pe.wait_ge(comb_done, nth(late, 1, 1))
                    nc.tensor.transpose(ps2[0:E * TILES, 0:P], comb_tm[:].rearrange("p e t -> p (e t)"), ident[:])\
                        .then_inc(comb_turned, 1)

            run(pe, slot)
            turn_gated(Group(BATCHES - 1, 1))

def kernel(**inputs):
    import numpy as np
    import concourse.bacc as bacc
    from concourse import mybir as mb
    from concourse.bass_utils import run_bass_kernel_spmd

    def a(name):
        return np.asarray(inputs["L0_" + name])

    x = a("attn_x")
    B, S, C = x.shape
    groups = B * S // TOK
    E, F, _ = a("ffn_w1").shape
    arrays = {
        "x": x.reshape(groups, TILES, P, C).transpose(0, 2, 1, 3).reshape(groups, P, TOK),
        "cT": a("c").T,
        "wmod": a("wmod"),
        "wq": a("attn_Wq"), "wk": a("attn_Wk"), "wv": a("attn_Wv"), "wbeta": a("attn_Wbeta"),
        "b_beta": a("attn_b_beta"), "wo": a("attn_Wo"), "b_o": a("attn_b_o"),
        "ln_g": a("attn_ln_g"), "ln_b": a("attn_ln_b"),
        "gamma": a("ffn_ln_gamma"), "beta_": a("ffn_ln_beta"),
        "gateT": a("ffn_gate_w").T,
        "w1T": a("ffn_w1").transpose(2, 0, 1).reshape(C, E * F),
        "w2T": a("ffn_w2").reshape(E, C, F // P, P).transpose(3, 0, 2, 1),
    }
    arrays = {n: np.ascontiguousarray(v) for n, v in arrays.items()}
    nc = bacc.Bacc("TRN2", target_bir_lowering=False, num_devices=1)
    args = [nc.dram_tensor("in_" + n, v.shape, mb.dt.from_np(v.dtype), kind="ExternalInput").ap()
            for n, v in arrays.items()]
    out = nc.dram_tensor("out", (groups, P, TOK), mb.dt.float32, kind="ExternalOutput").ap()
    adaln_moe_kernel(nc, *args, out)
    r = run_bass_kernel_spmd(nc, [{"in_" + n: v for n, v in arrays.items()}], core_ids=[0])
    got = r.results[0]["out"]
    return got.reshape(groups, P, TILES, C).transpose(0, 2, 1, 3).reshape(B, S, C)
```

```python
from contextlib import ExitStack

import concourse.bass as bass
from concourse import mybir

F32 = mybir.dt.float32
F32R = mybir.dt.float32r
U32 = mybir.dt.uint32
ALU = mybir.AluOpType
ACT = mybir.ActivationFunctionType
AX_X = mybir.AxisListType.X

P = 128
TILES = 4
TOK = TILES * P
EPS = 1e-5
GATE_FLOOR = 0.25
EXP_SQUARINGS = 2
SPLIT = (0, 1, 3)


class Group:

    def __init__(self, b, k):
        self.b, self.k = b, k

    def __add__(self, n):
        return Group(self.b, self.k + n)

    def __sub__(self, n):
        return Group(self.b, self.k - n)

    @property
    def slot(self):
        return self.k % 2

    @property
    def number(self):
        return 2 * self.b + self.k

    @property
    def batch(self):
        return self.b + self.k // 2


def exists(group):
    return not isinstance(group.b, int) or group.number >= 0


def nth(group, per, n):
    return (2 * per) * group.b + (per * group.k + n)


def turn(group, by=16):
    return by * group.b + by * (group.k // 2 + 1)


def adaln_moe_kernel(nc, x, cT, wmod, wq, wk, wv, wbeta, b_beta, wo, vectors, gateT,
                     w1T, w2T, out):
    GROUPS = x.shape[0]
    BATCHES = cT.shape[1]
    HEADS = wbeta.shape[1]
    D = P // HEADS
    E = gateT.shape[1]
    assert GROUPS == 2 * BATCHES and E == 8

    with ExitStack() as ctx:
        def sb(name, shape, dt=F32):
            return ctx.enter_context(nc.sbuf_tensor(name, shape, dt))

        def psum(name, shape):
            return ctx.enter_context(nc.psum_tensor(name, shape, F32))

        def sem(name):
            return ctx.enter_context(nc.semaphore(name))

        up_ps = psum("up_ps", [P, 3, TOK])
        down_ps = psum("down_ps", [P, 2, TOK])
        ps0 = psum("ps0", [P, TOK])
        ps1 = psum("ps1", [P, TOK])
        ps2 = psum("ps2", [P, TOK])

        W2_SPLIT = max(SPLIT) + 1
        ident = sb("ident", [P, P])
        minus_half = sb("minus_half", [P, TILES])
        half = sb("half", [P, 1])
        table_warm = sb("table_warm", [P, TILES])
        expert_ids = sb("expert_ids", [P, TILES, E])
        w1 = sb("w1", [P, E * 256])
        w1_hi = sb("w1_hi", [P, E * 256], F32R)
        w1_lo = sb("w1_lo", [P, E * 256], F32R)
        w2 = sb("w2", [P, E, 2, P])
        w2_hi = sb("w2_hi", [P, W2_SPLIT, 2, P], F32R)
        w2_lo = sb("w2_lo", [P, W2_SPLIT, 2, P], F32R)
        attn_w = sb("attn_w", [P, 5, P])
        attn_hi = sb("attn_hi", [P, 5, P], F32R)
        attn_lo = sb("attn_lo", [P, 5, P], F32R)
        Q, K, V, BETA, OUT = range(5)
        wq_sb = sb("wq_sb", [P, P])
        wv_sb = sb("wv_sb", [P, P])
        wbeta_sb = sb("wbeta_sb", [P, HEADS])
        head_sums = sb("head_sums", [P, 2, HEADS])
        cols = sb("cols", [P, 6])
        half_b_beta = sb("half_b_beta", [P, 1])
        gate = sb("gate", [P, E])
        gate_gamma = sb("gate_gamma", [P, E])
        gate_mid = sb("gate_mid", [P, E])
        gate_split_w = sb("gate_split_w", [P, 2, E], F32R)
        gate_bias = sb("gate_bias", [P, E])
        mean_w = sb("mean_w", [P, P])
        wmod_sb = sb("wmod_sb", [P, 6 * P])
        c_sb = sb("c_sb", [P, BATCHES])
        c_tanh = sb("c_tanh", [P, BATCHES])
        c_sig = sb("c_sig", [P, BATCHES])
        silu_c = sb("silu_c", [P, BATCHES])
        mods = sb("mods", [P, 6, BATCHES])
        sign = sb("sign", [P, 2, BATCHES])
        size = sb("size", [P, 2, BATCHES])
        gates = sb("gates", [P, 2, BATCHES])
        row_cols = sb("row_cols", [P, BATCHES, 4])
        scale_h = sb("scale_h", [P, BATCHES])
        rows = sb("rows", [P, BATCHES, 4, P])
        SCALE_A, SHIFT_A, SCALE_B, SHIFT_B = range(4)

        x_tm = sb("x_tm", [P, 2, TOK])
        ln1_bn = sb("ln1_bn", [P, TILES, 6])
        ln1_mv = sb("ln1_mv", [P, TILES, 2])
        ln1_ve = sb("ln1_ve", [P, TILES])
        ln1_r = sb("ln1_r", [P, TILES])
        ln1_neg = sb("ln1_neg", [P, TILES])
        ln1_nmr = sb("ln1_nmr", [P, TILES])
        n1_tm = sb("n1_tm", [P, TOK])
        h_cm = sb("h_cm", [P, TOK])
        h_hi = sb("h_hi", [P, TOK], F32R)
        h_lo = sb("h_lo", [P, TOK], F32R)
        beta_tanh = sb("beta_tanh", [P, TOK])
        beta_cm = sb("beta_cm", [P, TOK])
        vsum_cm = sb("vsum_cm", [P, TOK])
        kv_cm = sb("kv_cm", [P, TOK])
        state_cm = sb("state_cm", [P, 2, TOK])
        o_cm = sb("o_cm", [P, TOK])
        o_hi = sb("o_hi", [P, TOK], F32R)
        o_lo = sb("o_lo", [P, TOK], F32R)
        z_cm = sb("z_cm", [P, TOK])
        xb_tm = sb("xb_tm", [P, 2, TOK])

        lnz_bn = sb("lnz_bn", [P, TILES, 6])
        lnz_mv = sb("lnz_mv", [P, TILES, 2])
        lnz_ve = sb("lnz_ve", [P, TILES])
        lnz_r = sb("lnz_r", [P, TILES])
        lnz_neg = sb("lnz_neg", [P, TILES])
        lnz_nmr = sb("lnz_nmr", [P, TILES])
        nz_tm = sb("nz_tm", [P, TOK])
        nza_tm = sb("nza_tm", [P, TOK])
        x2_tm = sb("x2_tm", [P, 4 * TOK])
        ln2_bn = sb("ln2_bn", [P, TILES, 6])
        ln2_mv = sb("ln2_mv", [P, TILES, 2])
        ln2_ve = sb("ln2_ve", [P, TILES])
        ln2_r = sb("ln2_r", [P, TILES])
        n2_tm = sb("n2_tm", [P, TOK])
        n2c_tm = sb("n2c_tm", [P, TOK])
        h2_tm = sb("h2_tm", [P, TOK])
        ln3_bn = sb("ln3_bn", [P, TILES, 6])
        ln3_mv = sb("ln3_mv", [P, TILES, 2])
        ln3_ve = sb("ln3_ve", [P, TILES])
        ln3_r = sb("ln3_r", [P, TILES])
        raw_logits = sb("raw_logits", [P, TILES, E])
        scaled_logits = sb("scaled_logits", [P, TILES, E])
        logits = sb("logits", [P, TILES, E])
        top = sb("top", [P, TILES, 8])
        top_ids = sb("top_ids", [P, TILES, 8], U32)
        below = sb("below", [P, TILES, E])
        exp_tanh = sb("exp_tanh", [P, TILES, E])
        exp_den = sb("exp_den", [P, TILES, E])
        exp_rec = sb("exp_rec", [P, TILES, E])
        powers = sb("powers", [P, EXP_SQUARINGS + 1, TILES, E])
        is_first = sb("is_first", [P, TILES, E])
        is_second = sb("is_second", [P, TILES, E])
        chosen = sb("chosen", [P, TILES, E])
        exp_sum = sb("exp_sum", [P, TILES])
        exp_sum_rec = sb("exp_sum_rec", [P, TILES])
        exp_chosen = sb("exp_chosen", [P, TILES, E])
        comb_tm = sb("comb_tm", [P, E, TILES])
        comb_em = sb("comb_em", [E * TILES, P])
        comb_row = sb("comb_row", [1, E * TOK])
        h2_hi = sb("h2_hi", [P, 2, TOK], F32R)
        h2_lo = sb("h2_lo", [P, 2, TOK], F32R)

        comb_cm = sb("comb_cm", [P, 4, TOK])
        gelu_cm = sb("gelu_cm", [P, 2, 2, TOK])
        gelu_hi = sb("gelu_hi", [P, 2, 2, TOK], F32R)
        gelu_lo = sb("gelu_lo", [P, 2, 2, TOK], F32R)
        scaled_cm = sb("scaled_cm", [P, 2, TOK])
        sum_cm = sb("sum_cm", [P, 2, TOK])
        gated_cm = sb("gated_cm", [P, TOK])
        out_tm = sb("out_tm", [P, 2, TOK])

        s_weights = {n: sem("loaded_" + n) for n in
                     ("c", "wmod", "wq", "wk", "wv", "wbeta", "wo", "cols", "gate", "w1", "w2")}
        x_loaded = [sem("x_loaded0"), sem("x_loaded1")]
        row_loaded = sem("row_loaded")
        stored = [sem("stored0"), sem("stored1")]
        ident_zero = sem("ident_zero")
        consts = sem("consts")
        setup_step = sem("setup_step")
        silu_tanh_done = sem("silu_tanh_done")
        silu_done = sem("silu_done")
        mods_ps_done = sem("mods_ps_done")
        mod_cols_done = sem("mod_cols_done")
        half_b_beta_done = sem("half_b_beta_done")
        attn_split = sem("attn_split")
        row_cols_done = sem("row_cols_done")
        gates_done = sem("gates_done")
        gate_gamma_done = sem("gate_gamma_done")
        gate_ps_done = sem("gate_ps_done")
        gate_split = sem("gate_split")
        rows_ps_done = sem("rows_ps_done")
        rows_done = sem("rows_done")
        w1_hi_done = sem("w1_hi_done")
        w2_hi_done = sem("w2_hi_done")
        w1_split = sem("w1_split")
        w2_split = sem("w2_split")
        ln1_bn_done = sem("ln1_bn_done")
        ln1_mv_done = sem("ln1_mv_done")
        ln1_ve_done = sem("ln1_ve_done")
        ln1_r_done = sem("ln1_r_done")
        ln1_neg_done = sem("ln1_neg_done")
        ln1_nmr_done = sem("ln1_nmr_done")
        n1_done = sem("n1_done")
        n1_turned = sem("n1_turned")
        h_done = sem("h_done")
        h_hi_done = sem("h_hi_done")
        h_lo_done = sem("h_lo_done")
        beta_ps_done = sem("beta_ps_done")
        v_ps_done = sem("v_ps_done")
        k_ps_done = sem("k_ps_done")
        q_ps_done = sem("q_ps_done")
        beta_tanh_done = sem("beta_tanh_done")
        vsum_done = sem("vsum_done")
        beta_done = sem("beta_done")
        kv_done = sem("kv_done")
        scan_done = sem("scan_done")
        o_done = sem("o_done")
        o_hi_done = sem("o_hi_done")
        o_lo_done = sem("o_lo_done")
        out_ps_done = sem("out_ps_done")
        z_done = sem("z_done")
        xb_done = sem("xb_done")
        z_turned = sem("z_turned")
        lnz_bn_done = sem("lnz_bn_done")
        lnz_mv_done = sem("lnz_mv_done")
        lnz_ve_done = sem("lnz_ve_done")
        lnz_r_done = sem("lnz_r_done")
        lnz_neg_done = sem("lnz_neg_done")
        lnz_nmr_done = sem("lnz_nmr_done")
        nz_done = sem("nz_done")
        nza_done = sem("nza_done")
        x2_done = sem("x2_done")
        ln2_bn_done = sem("ln2_bn_done")
        ln2_mv_done = sem("ln2_mv_done")
        ln2_ve_done = sem("ln2_ve_done")
        ln2_r_done = sem("ln2_r_done")
        n2_done = sem("n2_done")
        n2c_done = sem("n2c_done")
        h2_done = sem("h2_done")
        ln3_bn_done = sem("ln3_bn_done")
        ln3_mv_done = sem("ln3_mv_done")
        ln3_ve_done = sem("ln3_ve_done")
        ln3_r_done = sem("ln3_r_done")
        logits_ps_done = sem("logits_ps_done")
        logits_read = sem("logits_read")
        logits_scaled = sem("logits_scaled")
        logits_done = sem("logits_done")
        top_done = sem("top_done")
        below_done = sem("below_done")
        exp_tanh_done = sem("exp_tanh_done")
        top_ids_done = sem("top_ids_done")
        den_done = sem("den_done")
        is_top_done = sem("is_top_done")
        rec_done = sem("rec_done")
        chosen_done = sem("chosen_done")
        root_done = sem("root_done")
        squared = sem("squared")
        exp_chosen_done = sem("exp_chosen_done")
        exp_sum_done = sem("exp_sum_done")
        exp_sum_rec_done = sem("exp_sum_rec_done")
        comb_done = sem("comb_done")
        comb_turned = sem("comb_turned")
        comb_em_done = sem("comb_em_done")
        comb_spread = sem("comb_spread")
        h2_turned = sem("h2_turned")
        h2_hi_done = sem("h2_hi_done")
        h2_lo_done = sem("h2_lo_done")
        up_done = sem("up_done")
        gelu_done = sem("gelu_done")
        gelu_hi_done = sem("gelu_hi_done")
        gelu_lo_done = sem("gelu_lo_done")
        down_done = sem("down_done")
        scaled_done = sem("scaled_done")
        sum_done = sem("sum_done")
        gated_done = sem("gated_done")
        gated_turned = sem("gated_turned")
        out_done = sem("out_done")

        block = ctx.enter_context(nc.Block())

        def run(engine, slot):
            def step(experts, late, early):
                for s in range(E):
                    slot(s, experts, late, early)

            step(None, None, Group(0, 0))
            step(None, Group(0, 0), Group(0, 1))
            for k in range(2):
                step(Group(0, k), Group(0, k + 1), Group(0, k + 2))
            with engine.Fori(1, BATCHES - 2) as b:
                for k in range(2):
                    step(Group(b, k), Group(b, k + 1), Group(b, k + 2))
            for k in range(2):
                step(Group(BATCHES - 2, k), Group(BATCHES - 2, k + 1), Group(BATCHES - 2, k + 2))
            last = BATCHES - 1
            step(Group(last, 0), Group(last, 1), None)
            step(Group(last, 1), None, None)

        def tile(t):
            return slice(t * P, (t + 1) * P)

        def tiles_of(rows):
            return lambda t: rows[:, tile(t)]

        CHUNKS = 2 * E
        UP_BANK = [0, 1, 2] * 5 + [1]

        def chunk_before(c):
            for back in range(1, CHUNKS):
                if UP_BANK[(c - back) % CHUNKS] == UP_BANK[c]:
                    return (c - back) % CHUNKS, int(c < back)

        split_before = [sum(e < n for e in SPLIT) for n in range(E + 1)]
        NS = len(SPLIT)

        def first_of_all(g):
            return isinstance(g.b, int) and g.number == 0

        def has_next(g):
            return not (isinstance(g.b, int) and g.number + 1 >= GROUPS)

        def row_of(which, g, tiles=None):
            batch = g.batch
            if tiles is None:
                start = batch * (4 * P) + which * P
                flat = rows[:].rearrange("p b w c -> p (b w c)")
                return flat[:, start:start + P] if isinstance(start, int) else flat[:, bass.ds(start, P)]
            at = slice(batch, batch + 1) if isinstance(batch, int) else bass.ds(batch, 1)
            return rows[:, at, which, :].broadcast_to([P, TILES, P])

        def batch_col(cols_of_batches, g):
            batch = g.batch
            return cols_of_batches[:, batch:batch + 1] if isinstance(batch, int) \
                else cols_of_batches[:, bass.ds(batch, 1)]

        def x2_of(g, first=0, width=TOK):
            start = (g.batch % 2) * (2 * TOK) + (g.slot * TOK + first)
            return x2_tm[:, start:start + width] if isinstance(start, int) else x2_tm[:, bass.ds(start, width)]

        def settle(engine):
            engine.nop(nofuse=True)

        def by_tile(rows):
            return rows.rearrange("p (t c) -> p t c", t=TILES)

        def row_bank(b):
            return down_ps[:, b % 2, :]

        def gb_of(g):
            return batch_col(gates[:, 1, :], g)

        @block.sync
        def _(sp):
            def load_x(g):
                if exists(g - 2):
                    sp.wait_ge(n1_done, nth(g - 2, 1, 1))
                    settle(sp)
                    sp.wait_ge(xb_done, nth(g - 2, 1, 1))
                settle(sp)
                sp.dma_start(x_tm[:, g.slot, :], x[g.number]).then_inc(x_loaded[g.slot], 16)

            sp.dma_start(c_sb[:], cT).then_inc(s_weights["c"], 16)
            load_x(Group(0, 0))
            sp.dma_start(wmod_sb[:], wmod).then_inc(s_weights["wmod"], 16)
            sp.dma_start(wbeta_sb[:], wbeta).then_inc(s_weights["wbeta"], 16)
            sp.dma_start(wv_sb[:], wv).then_inc(s_weights["wv"], 16)
            sp.dma_start(attn_w[:, K, :], wk).then_inc(s_weights["wk"], 16)
            sp.dma_start(wq_sb[:], wq).then_inc(s_weights["wq"], 16)
            sp.dma_start(attn_w[:, OUT, :], wo).then_inc(s_weights["wo"], 16)
            load_x(Group(0, 1))
            sp.dma_start(w1[:], w1T).then_inc(s_weights["w1"], 16)
            sp.dma_start(w2[:], w2T).then_inc(s_weights["w2"], 16)

            def slot(s, experts, late, early):
                if s == 1 and early and has_next(early) and not first_of_all(early):
                    load_x(early + 1)
                if s == 0 and experts:
                    sp.wait_ge(comb_em_done, nth(experts, 1, 1))
                    settle(sp)
                    if exists(experts - 1):
                        sp.wait_ge(comb_spread, nth(experts - 1, E, E))
                        settle(sp)
                    sp.dma_start(comb_row[0:1, :], comb_em[:]).then_inc(row_loaded, 16)
                if s == 7 and experts and exists(experts - 1):
                    store(experts - 1)

            def store(g):
                sp.wait_ge(out_done, nth(g, 1, 1))
                settle(sp)
                sp.dma_start(out[g.number], out_tm[:, g.slot, :]).then_inc(stored[g.slot], 16)

            run(sp, slot)
            store(Group(BATCHES - 1, 1))
            for p in range(2):
                sp.wait_ge(stored[p], 16 * BATCHES)

        @block.gpsimd
        def _(pool):
            nc.gpsimd.memset(ident[:], 0.0).then_inc(ident_zero, 1)
            pool.wait_ge(ident_zero, 1)
            nc.gpsimd.affine_select(out=ident[:], in_=ident[:], compare_op=ALU.not_equal, fill=1.0, base=0,
                                    pattern=[[-1, P]], channel_multiplier=1).then_inc(consts, 1)
            nc.gpsimd.memset(minus_half[:], -0.5).then_inc(consts, 1)
            nc.gpsimd.iota(expert_ids[:], pattern=[[0, TILES], [1, E]], base=0, channel_multiplier=0,
                           allow_small_or_imprecise_dtypes=True).then_inc(consts, 1)
            nc.gpsimd.memset(mean_w[:], 1.0 / P).then_inc(consts, 1)
            nc.gpsimd.memset(half[:], 0.5).then_inc(consts, 1)
            pool.wait_ge(consts, 5)

            def rstd(g, mv, mv_done, ve, ve_done, r, r_done, r_used):
                pool.wait_ge(mv_done, nth(g, 1, 1))
                settle(pool)
                nc.gpsimd.tensor_scalar(ve[:], mv[:, :, 1], 1.0, EPS, ALU.mult, ALU.add).then_inc(ve_done, 1)
                pool.wait_ge(ve_done, nth(g, 1, 1))
                if exists(g - 1):
                    pool.wait_ge(r_used, nth(g - 1, 1, 1))
                nc.gpsimd.tensor_tensor(r[:], ve[:], minus_half[:], ALU.pow).then_inc(r_done, 1)

            def shift(g, mv, neg, neg_done, r, r_done, nmr, nmr_done):
                nc.gpsimd.tensor_scalar(neg[:], mv[:, :, 0], -1.0, 0.0, ALU.mult, ALU.add).then_inc(neg_done, 1)
                pool.wait_ge(neg_done, nth(g, 1, 1))
                settle(pool)
                pool.wait_ge(r_done, nth(g, 1, 1))
                nc.gpsimd.tensor_tensor(nmr[:], neg[:], r[:], ALU.mult).then_inc(nmr_done, 1)

            def ln1_scales(g):
                rstd(g, ln1_mv, ln1_mv_done, ln1_ve, ln1_ve_done, ln1_r, ln1_r_done, n1_done)
                shift(g, ln1_mv, ln1_neg, ln1_neg_done, ln1_r, ln1_r_done, ln1_nmr, ln1_nmr_done)

            def spread(g, e):
                if e == 0:
                    pool.wait_ge(row_loaded, nth(g, 16, 16))
                if e >= 4:
                    pool.wait_ge(scaled_done, nth(g, E, e - 3))
                elif exists(g - 1):
                    pool.wait_ge(scaled_done, nth(g - 1, E, e + 5))
                settle(pool)
                nc.gpsimd.partition_broadcast(comb_cm[:, e % 4, :], comb_row[0:1, e * TOK:(e + 1) * TOK], P)\
                    .then_inc(comb_spread, 1)

            def add_expert(g, e):
                pool.wait_ge(scaled_done, nth(g, E, e + 1))
                if e >= 2:
                    pool.wait_ge(sum_done, nth(g, E - 1, e - 1))
                nc.gpsimd.tensor_tensor(sum_cm[:, g.slot, :], sum_cm[:, g.slot, :], scaled_cm[:, e % 2, :], ALU.add)\
                    .then_inc(sum_done, 1)

            def slot(s, experts, late, early):
                if experts and s == 0 and exists(experts - 1):
                    add_expert(experts - 1, E - 1)
                if late:
                    if s == 0:
                        rstd(late, lnz_mv, lnz_mv_done, lnz_ve, lnz_ve_done, lnz_r, lnz_r_done, nz_done)
                        shift(late, lnz_mv, lnz_neg, lnz_neg_done, lnz_r, lnz_r_done, lnz_nmr, lnz_nmr_done)
                    if s == 2:
                        rstd(late, ln2_mv, ln2_mv_done, ln2_ve, ln2_ve_done, ln2_r, ln2_r_done, n2_done)
                if early and s == 1:
                    pool.wait_ge(h_hi_done, nth(early, 1, 1))
                    if exists(early - 1):
                        pool.wait_ge(q_ps_done, nth(early - 1, 1, 1))
                    nc.gpsimd.tensor_tensor(h_lo[:], h_cm[:], h_hi[:].bitcast(F32), ALU.subtract)\
                        .then_inc(h_lo_done, 1)
                if experts:
                    if s == 0:
                        spread(experts, 0)
                    elif s == 1:
                        spread(experts, 1)
                        spread(experts, 2)
                    elif s < 7:
                        spread(experts, s + 1)
                    if s >= 2:
                        add_expert(experts, s - 1)
                if late and s == 4:
                    rstd(late, ln3_mv, ln3_mv_done, ln3_ve, ln3_ve_done, ln3_r, ln3_r_done, logits_scaled)
                if early:
                    if s == 4 and has_next(early):
                        ln1_scales(early + 1)
                    if s == (7 if first_of_all(early) else 5):
                        if first_of_all(early):
                            pool.wait_ge(rows_done, 1)
                        elif first_of_all(early - 2):
                            pool.wait_ge(rows_done, BATCHES)
                        if exists(early - 2):
                            pool.wait_ge(x2_done, nth(early - 2, 1, 1))
                        settle(pool)
                        nc.gpsimd.tensor_tensor(by_tile(xb_tm[:, early.slot, :]), by_tile(x_tm[:, early.slot, :]),
                                                row_of(SHIFT_A, early, TILES), ALU.add).then_inc(xb_done, 1)
                    if s == 5 and first_of_all(early):
                        pool.wait_ge(w2_hi_done, 1)
                        nc.gpsimd.tensor_tensor(w2_lo[:], w2[:, 0:W2_SPLIT], w2_hi[:].bitcast(F32), ALU.subtract)\
                            .then_inc(w2_split, 1)

            ln1_scales(Group(0, 0))
            run(pool, slot)
            add_expert(Group(BATCHES - 1, 1), E - 1)

        @block.scalar
        def _(act):
            act.dma_start(cols[:, 1:6], vectors).then_inc(s_weights["cols"], 16)
            act.dma_start(cols[:, 0:1], b_beta.rearrange("(h o) -> h o", o=1).broadcast_to([HEADS, D]))\
                .then_inc(s_weights["cols"], 16)
            act.dma_start(gate[:], gateT).then_inc(s_weights["gate"], 16)
            act.wait_ge(consts, 5)
            nc.scalar.activation(table_warm[:], minus_half[:], ACT.Gelu)
            act.wait_ge(s_weights["c"], 16)
            nc.scalar.activation(c_tanh[:], c_sb[:], ACT.Tanh, scale=0.5).then_inc(silu_tanh_done, 1)

            def first_norm(g):
                act.wait_ge(ln1_nmr_done, nth(g, 1, 1))
                if exists(g - 1):
                    act.wait_ge(n1_turned, nth(g - 1, 1, 1))
                normalize(n1_tm, tiles_of(x_tm[:, g.slot, :]), ln1_r, ln1_nmr, n1_done)

            def normalize(dst, src, r, nmr, done):
                for t in range(TILES):
                    ins = nc.scalar.activation(dst[:, tile(t)], src(t), ACT.Identity, scale=r[:, t:t + 1],
                                               bias=nmr[:, t:t + 1])
                ins.then_inc(done, 1)

            def gelu(g, e):
                for f in range(2):
                    c = 2 * e + f
                    act.wait_ge(up_done, nth(g, CHUNKS, c + 1))
                    if f == 0:
                        if e >= 2:
                            act.wait_ge(down_done, nth(g, E, e - 1))
                        elif exists(g - 1):
                            act.wait_ge(down_done, nth(g - 1, E, e + 7))
                    if e in SPLIT:
                        nc.scalar.activation(gelu_hi[:, e % 2, f, :], up_ps[:, UP_BANK[c], :], ACT.Gelu)\
                            .then_inc(gelu_hi_done, 1)
                    nc.scalar.activation(gelu_cm[:, e % 2, f, :], up_ps[:, UP_BANK[c], :], ACT.Gelu)\
                        .then_inc(gelu_done, 1)

            def gate_sum(g):
                act.wait_ge(sum_done, nth(g, E - 1, E - 1))
                if exists(g - 1):
                    act.wait_ge(gated_turned, nth(g - 1, 1, 1))
                settle(act)
                nc.scalar.activation(gated_cm[:], sum_cm[:, g.slot, :], ACT.Copy, scale=gb_of(g))\
                    .then_inc(gated_done, 1)

            def copy_rows(b):
                act.wait_ge(rows_ps_done, b + 1)
                nc.scalar.activation(rows[:, b].rearrange("p w c -> p (w c)"), row_bank(b), ACT.Copy)\
                    .then_inc(rows_done, 1)

            def slot(s, experts, late, early):
                if late and first_of_all(late) and s < BATCHES - 1:
                    copy_rows(s + 1)
                if s == 7 and late:
                    act.wait_ge(root_done, nth(late, 1, 1))
                    for n in range(EXP_SQUARINGS):
                        if n:
                            act.wait_ge(squared, nth(late, EXP_SQUARINGS, n))
                        elif exists(late - 1):
                            act.wait_ge(exp_sum_done, nth(late - 1, 1, 1))
                        nc.scalar.activation(powers[:, n + 1], powers[:, n], ACT.Square).then_inc(squared, 1)
                if experts and s == 0:
                    act.wait_ge(comb_turned, nth(experts, 1, 1))
                    if exists(experts - 1):
                        act.wait_ge(row_loaded, nth(experts - 1, 16, 16))
                    nc.scalar.activation(comb_em[:], ps2[0:E * TILES, 0:P], ACT.Copy).then_inc(comb_em_done, 1)
                if experts and s < 7:
                    gelu(experts, s + 1)
                if s == 7 and late:
                    gelu(late, 0)
                if late and s == 1:
                    act.wait_ge(lnz_nmr_done, nth(late, 1, 1))
                    if exists(late - 1):
                        act.wait_ge(nza_done, nth(late - 1, 1, 1))
                    normalize(nz_tm, tiles_of(ps1), lnz_r, lnz_nmr, nz_done)
                if early and s == 6 and has_next(early):
                    first_norm(early + 1)
                if s == 5 and experts and exists(experts - 1):
                    gate_sum(experts - 1)
                if early:
                    if s == 0:
                        act.wait_ge(n1_turned, nth(early, 1, 1))
                        if first_of_all(early):
                            act.wait_ge(mod_cols_done, 1)
                        if exists(early - 1):
                            act.wait_ge(z_done, nth(early - 1, 1, 1))
                        settle(act)
                        nc.scalar.activation(h_cm[:], ps0[:], ACT.Identity, scale=batch_col(scale_h[:], early),
                                             bias=batch_col(mods[:, 0, :], early)).then_inc(h_done, 1)
                        act.wait_ge(h_done, nth(early, 1, 1))
                        if exists(early - 1):
                            act.wait_ge(q_ps_done, nth(early - 1, 1, 1))
                        nc.scalar.activation(h_hi[:], h_cm[:], ACT.Copy).then_inc(h_hi_done, 1)
                        if first_of_all(early):
                            act.wait_ge(s_weights["w1"], 16)
                            nc.scalar.activation(w1_hi[:], w1[:], ACT.Copy).then_inc(w1_hi_done, 1)
                    if s == 2:
                        act.wait_ge(v_ps_done, nth(early, 1, 1))
                        if exists(early - 1):
                            act.wait_ge(kv_done, nth(early - 1, 1, 1))
                        nc.scalar.activation(vsum_cm[:], ps0[:], ACT.Copy).then_inc(vsum_done, 1)
                        act.wait_ge(beta_ps_done, nth(early, 1, 1))
                        if first_of_all(early):
                            act.wait_ge(half_b_beta_done, 1)
                        if exists(early - 1):
                            act.wait_ge(beta_done, nth(early - 1, 1, 1))
                        nc.scalar.activation(beta_tanh[:], ps1[:], ACT.Tanh, scale=0.5, bias=half_b_beta[:])\
                            .then_inc(beta_tanh_done, 1)
                        act.wait_ge(beta_tanh_done, nth(early, 1, 1))
                        if exists(early - 1):
                            act.wait_ge(scan_done, nth(early - 1, 1, 1))
                        nc.scalar.activation(beta_cm[:], beta_tanh[:], ACT.Identity, scale=0.5, bias=half[:])\
                            .then_inc(beta_done, 1)
                        if first_of_all(early):
                            act.wait_ge(s_weights["w2"], 16)
                            nc.scalar.activation(w2_hi[:], w2[:, 0:W2_SPLIT], ACT.Copy).then_inc(w2_hi_done, 1)
                    if s == 5:
                        act.wait_ge(o_done, nth(early, 1, 1))
                        if exists(early - 1):
                            act.wait_ge(out_ps_done, nth(early - 1, 1, 1))
                        nc.scalar.activation(o_hi[:], o_cm[:], ACT.Copy).then_inc(o_hi_done, 1)
                        if first_of_all(early):
                            copy_rows(0)
                if late:
                    if s == 4:
                        act.wait_ge(h2_turned, nth(late, 1, 1))
                        if exists(late - 2):
                            act.wait_ge(up_done, nth(late - 2, CHUNKS, CHUNKS))
                        nc.scalar.activation(h2_hi[:, late.slot, :], ps2[:], ACT.Copy).then_inc(h2_hi_done, 1)
                    if s == 6:
                        act.wait_ge(below_done, nth(late, 1, 1))
                        if exists(late - 1):
                            act.wait_ge(root_done, nth(late - 1, 1, 1))
                        nc.scalar.activation(exp_tanh[:], below[:], ACT.Tanh, scale=0.5 / 2 ** EXP_SQUARINGS)\
                            .then_inc(exp_tanh_done, 1)

            first_norm(Group(0, 0))
            run(act, slot)
            gate_sum(Group(BATCHES - 1, 1))

        @block.vector
        def _(dve):
            done = [0]

            def then(ins):
                done[0] += 1
                ins.then_inc(setup_step, 1)
                dve.wait_ge(setup_step, done[0])

            def first_stats(g):
                dve.wait_ge(x_loaded[g.slot], turn(g))
                stats(g, tiles_of(x_tm[:, g.slot, :]), ln1_bn, ln1_bn_done, ln1_mv, ln1_mv_done, ln1_nmr_done)

            def stats(g, src, bn, bn_done, mv, mv_done, mv_used):
                settle(dve)
                for t in range(TILES):
                    ins = nc.vector.bn_stats(bn[:, t, :], src(t))
                ins.then_inc(bn_done, 1)
                dve.wait_ge(bn_done, nth(g, 1, 1))
                if exists(g - 1):
                    dve.wait_ge(mv_used, nth(g - 1, 1, 1))
                settle(dve)
                for t in range(TILES):
                    ins = nc.vector.bn_aggr(mv[:, t, :], bn[:, t, :])
                ins.then_inc(mv_done, 1)

            first_stats(Group(0, 0))
            dve.wait_ge(silu_tanh_done, 1)
            then(nc.vector.tensor_scalar(c_sig[:], c_tanh[:], 0.5, 0.5, ALU.mult, ALU.add))
            nc.vector.tensor_tensor(silu_c[:], c_sb[:], c_sig[:], ALU.mult).then_inc(silu_done, 1)
            dve.wait_ge(s_weights["cols"], 32)
            nc.vector.tensor_scalar(half_b_beta[:], cols[:, 0:1], 0.5, None, ALU.mult).then_inc(half_b_beta_done, 1)

            def by_head(row):
                return row.rearrange("p (h d) -> p h d", h=HEADS)

            def repeated(row):
                return row.rearrange("p (h o) -> p h o", o=1).broadcast_to([P, HEADS, D])

            dve.wait_ge(s_weights["wbeta"], 16)
            nc.vector.tensor_copy(by_head(attn_w[:, BETA, :]), repeated(wbeta_sb[:]))
            dve.wait_ge(s_weights["wv"], 16)
            nc.vector.tensor_reduce(head_sums[:, 0, :], by_head(wv_sb[:]), AX_X, ALU.add)
            dve.wait_ge(mods_ps_done, 1)
            nc.vector.tensor_copy(mods[:, 0, :], ps0[:, 0:BATCHES])
            nc.vector.tensor_scalar(scale_h[:], ps0[:, BATCHES:2 * BATCHES], 1.0, None, ALU.add)\
                .then_inc(mod_cols_done, 1)
            dve.wait_ge(s_weights["wq"], 16)
            then(nc.vector.tensor_reduce(head_sums[:, 1, :], by_head(wq_sb[:]), AX_X, ALU.add))
            nc.vector.tensor_copy(by_head(attn_w[:, V, :]), repeated(head_sums[:, 0, :]))
            then(nc.vector.tensor_copy(by_head(attn_w[:, Q, :]), repeated(head_sums[:, 1, :])))
            dve.wait_ge(s_weights["wk"], 16)
            dve.wait_ge(s_weights["wo"], 16)
            then(nc.vector.tensor_copy(attn_hi[:], attn_w[:]))
            nc.vector.tensor_tensor(attn_lo[:], attn_w[:], attn_hi[:].bitcast(F32), ALU.subtract)\
                .then_inc(attn_split, 1)
            dve.wait_ge(mods_ps_done, 2)
            then(nc.vector.tensor_copy(mods[:, 2:].rearrange("p j b -> p (j b)"), ps2[:, 2 * BATCHES:6 * BATCHES]))
            gagb = mods[:, 2:6:3, :]
            then(nc.vector.tensor_scalar(sign[:], gagb, 0.0, 2.0, ALU.is_ge, ALU.mult))
            then(nc.vector.tensor_scalar(sign[:], sign[:], -1.0, None, ALU.add))
            then(nc.vector.tensor_tensor(size[:], gagb, sign[:], ALU.mult))
            nc.vector.scalar_tensor_tensor(out=gates[:], in0=size[:], scalar=GATE_FLOOR, in1=sign[:],
                                           op0=ALU.max, op1=ALU.mult).then_inc(gates_done, 1)
            nc.vector.tensor_scalar(row_cols[:, :, SCALE_B], mods[:, 4, :], 1.0, None, ALU.add)
            nc.vector.tensor_copy(row_cols[:, :, SHIFT_B], mods[:, 3, :])
            dve.wait_ge(gates_done, 1)
            nc.vector.tensor_scalar(row_cols[:, :, SCALE_A], gates[:, 0, :], cols[:, 4:5], None, ALU.mult)
            nc.vector.tensor_scalar(row_cols[:, :, SHIFT_A], gates[:, 0, :], cols[:, 5:6], None, ALU.mult)\
                .then_inc(row_cols_done, 1)
            dve.wait_ge(s_weights["gate"], 16)
            nc.vector.tensor_scalar(gate_gamma[:], gate[:], cols[:, 2:3], None, ALU.mult).then_inc(gate_gamma_done, 1)
            dve.wait_ge(consts, 5)

            def scale_expert(g, e):
                dve.wait_ge(down_done, nth(g, E, e + 1))
                dve.wait_ge(comb_spread, nth(g, E, e + 1))
                if e == 0:
                    if exists(g - 2):
                        dve.wait_ge(gated_done, nth(g - 2, 1, 1))
                    dst = sum_cm[:, g.slot, :]
                else:
                    if e >= 3:
                        dve.wait_ge(sum_done, nth(g, E - 1, e - 2))
                    elif exists(g - 1):
                        dve.wait_ge(sum_done, nth(g - 1, E - 1, 6 if e == 2 else 7))
                    dst = scaled_cm[:, e % 2, :]
                nc.vector.tensor_tensor(dst, down_ps[:, e % 2, :], comb_cm[:, e % 4, :], ALU.mult)\
                    .then_inc(scaled_done, 1)

            def gelu_low(g, e):
                dve.wait_ge(gelu_done, nth(g, CHUNKS, 2 * e + 2))
                dve.wait_ge(gelu_hi_done, nth(g, 2 * NS, 2 * split_before[e] + 2))
                nc.vector.tensor_tensor(gelu_lo[:, e % 2], gelu_cm[:, e % 2], gelu_hi[:, e % 2].bitcast(F32),
                                        ALU.subtract).then_inc(gelu_lo_done, 1)

            def add_residual(g):
                dve.wait_ge(gated_turned, nth(g, 1, 1))
                if exists(g - 2):
                    dve.wait_ge(stored[g.slot], turn(g - 2))
                nc.vector.tensor_tensor(out_tm[:, g.slot, :], ps0[:], x2_of(g), ALU.add)\
                    .then_inc(out_done, 1)

            def early_work(s, early):
                if s == 4:
                    dve.wait_ge(k_ps_done, nth(early, 1, 1))
                    dve.wait_ge(vsum_done, nth(early, 1, 1))
                    nc.vector.tensor_tensor(kv_cm[:], ps1[:], vsum_cm[:], ALU.mult).then_inc(kv_done, 1)
                    dve.wait_ge(beta_done, nth(early, 1, 1))
                    dve.wait_ge(kv_done, nth(early, 1, 1))
                    if exists(early - 2):
                        dve.wait_ge(o_done, nth(early - 2, 1, 1))
                    start = 0.0 if early.slot == 0 else state_cm[:, 0, TOK - 1:TOK]
                    nc.vector.tensor_tensor_scan(state_cm[:, early.slot, :], beta_cm[:], kv_cm[:], start,
                                                 ALU.mult, ALU.add).then_inc(scan_done, 1)
                    dve.wait_ge(scan_done, nth(early, 1, 1))
                    dve.wait_ge(q_ps_done, nth(early, 1, 1))
                    if exists(early - 1):
                        dve.wait_ge(o_lo_done, nth(early - 1, 1, 1))
                    nc.vector.tensor_tensor(o_cm[:], ps0[:], state_cm[:, early.slot, :], ALU.mult)\
                        .then_inc(o_done, 1)
                if s == 5:
                    dve.wait_ge(o_hi_done, nth(early, 1, 1))
                    nc.vector.tensor_tensor(o_lo[:], o_cm[:], o_hi[:].bitcast(F32), ALU.subtract)\
                        .then_inc(o_lo_done, 1)
                if s == 2 and first_of_all(early):
                    dve.wait_ge(w1_hi_done, 1)
                    nc.vector.tensor_tensor(w1_lo[:], w1[:], w1_hi[:].bitcast(F32), ALU.subtract)\
                        .then_inc(w1_split, 1)
                if s == 7:
                    dve.wait_ge(out_ps_done, nth(early, 1, 1))
                    if exists(early - 1):
                        dve.wait_ge(z_turned, nth(early - 1, 1, 1))
                    nc.vector.scalar_tensor_tensor(out=z_cm[:], in0=ps1[:], scalar=cols[:, 1:2], in1=h_cm[:],
                                                   op0=ALU.add, op1=ALU.add).then_inc(z_done, 1)
                if s == 7 and first_of_all(early):
                    dve.wait_ge(gate_ps_done, 1)
                    then(nc.vector.tensor_tensor(gate_mid[:], gate_gamma[:], ps2[:, 0:E], ALU.subtract))
                    nc.vector.tensor_copy(gate_bias[:], ps2[:, E:2 * E])
                    then(nc.vector.tensor_copy(gate_split_w[:, 0, :], gate_mid[:]))
                    nc.vector.tensor_tensor(gate_split_w[:, 1, :], gate_mid[:], gate_split_w[:, 0, :].bitcast(F32),
                                            ALU.subtract).then_inc(gate_split, 1)

            def late_work(s, late):
                if s == 0:
                    dve.wait_ge(z_turned, nth(late, 1, 1))
                    stats(late, tiles_of(ps1), lnz_bn, lnz_bn_done, lnz_mv, lnz_mv_done, lnz_nmr_done)
                if s == 1:
                    dve.wait_ge(nz_done, nth(late, 1, 1))
                    if not exists(late - 1):
                        dve.wait_ge(rows_done, 1)
                    elif first_of_all(late - 1):
                        dve.wait_ge(rows_done, BATCHES)
                    nc.vector.tensor_tensor(by_tile(nza_tm[:]), by_tile(nz_tm[:]), row_of(SCALE_A, late, TILES),
                                            ALU.mult).then_inc(nza_done, 1)
                    dve.wait_ge(nza_done, nth(late, 1, 1))
                    dve.wait_ge(xb_done, nth(late, 1, 1))
                    nc.vector.tensor_tensor(x2_of(late), nza_tm[:], xb_tm[:, late.slot, :], ALU.add)\
                        .then_inc(x2_done, 1)
                if s == 2:
                    dve.wait_ge(x2_done, nth(late, 1, 1))
                    stats(late, lambda t: x2_of(late, t * P, P), ln2_bn, ln2_bn_done, ln2_mv, ln2_mv_done, n2_done)
                if s == 3:
                    dve.wait_ge(ln2_r_done, nth(late, 1, 1))
                    for t in range(TILES):
                        ins = nc.vector.tensor_scalar(n2_tm[:, tile(t)], x2_of(late, t * P, P), ln2_mv[:, t, 0:1],
                                                      ln2_r[:, t:t + 1], ALU.subtract, ALU.mult)
                    ins.then_inc(n2_done, 1)
                    dve.wait_ge(n2_done, nth(late, 1, 1))
                    nc.vector.tensor_tensor(by_tile(n2c_tm[:]), by_tile(n2_tm[:]), row_of(SCALE_B, late, TILES),
                                            ALU.mult).then_inc(n2c_done, 1)
                    dve.wait_ge(n2c_done, nth(late, 1, 1))
                    if exists(late - 1):
                        dve.wait_ge(h2_turned, nth(late - 1, 1, 1))
                    nc.vector.tensor_tensor(by_tile(h2_tm[:]), by_tile(n2c_tm[:]), row_of(SHIFT_B, late, TILES),
                                            ALU.add).then_inc(h2_done, 1)
                if s == 4:
                    dve.wait_ge(h2_done, nth(late, 1, 1))
                    stats(late, tiles_of(h2_tm), ln3_bn, ln3_bn_done, ln3_mv, ln3_mv_done, ln3_ve_done)
                if s == 6:
                    dve.wait_ge(logits_ps_done, nth(late, 1, 1))
                    dve.wait_ge(ln3_r_done, nth(late, 1, 1))
                    nc.vector.tensor_reduce(raw_logits[:], ps2[:, 0:2 * TILES * E]
                                            .rearrange("p (t w e) -> p t e w", w=2, e=E), AX_X, ALU.add)\
                        .then_inc(logits_read, 1)
                    dve.wait_ge(logits_read, nth(late, 1, 1))
                    nc.vector.tensor_tensor(scaled_logits[:], raw_logits[:],
                                            ln3_r[:].rearrange("p (t o) -> p t o", o=1).broadcast_to([P, TILES, E]),
                                            ALU.mult).then_inc(logits_scaled, 1)
                    dve.wait_ge(logits_scaled, nth(late, 1, 1))
                    nc.vector.tensor_tensor(logits[:], scaled_logits[:],
                                            gate_bias[:].rearrange("p (o e) -> p o e", o=1)
                                            .broadcast_to([P, TILES, E]), ALU.add).then_inc(logits_done, 1)
                    dve.wait_ge(logits_done, nth(late, 1, 1))
                    settle(dve)
                    for t in range(TILES):
                        ins = nc.vector.max(top[:, t, :], logits[:, t, :])
                    ins.then_inc(top_done, 1)
                    dve.wait_ge(top_done, nth(late, 1, 1))
                    nc.vector.tensor_tensor(below[:], logits[:], top[:, :, 0:1].broadcast_to([P, TILES, E]),
                                            ALU.subtract).then_inc(below_done, 1)
                    for t in range(TILES):
                        ins = nc.vector.max_index(top_ids[:, t, :], top[:, t, :], logits[:, t, :])
                    ins.then_inc(top_ids_done, 1)
                    dve.wait_ge(top_ids_done, nth(late, 1, 1))
                    nc.vector.tensor_tensor(is_first[:], expert_ids[:], top_ids[:, :, 0:1].broadcast_to([P, TILES, E]),
                                            ALU.is_equal)
                    nc.vector.tensor_tensor(is_second[:], expert_ids[:], top_ids[:, :, 1:2].broadcast_to([P, TILES, E]),
                                            ALU.is_equal).then_inc(is_top_done, 1)
                    dve.wait_ge(exp_tanh_done, nth(late, 1, 1))
                    nc.vector.tensor_scalar(exp_den[:], exp_tanh[:], -1.0, 1.0, ALU.mult, ALU.add).then_inc(den_done, 1)
                    dve.wait_ge(is_top_done, nth(late, 1, 1))
                    nc.vector.tensor_tensor(chosen[:], is_first[:], is_second[:], ALU.add).then_inc(chosen_done, 1)
                    dve.wait_ge(den_done, nth(late, 1, 1))
                    nc.vector.reciprocal(exp_rec[:], exp_den[:]).then_inc(rec_done, 1)
                    dve.wait_ge(rec_done, nth(late, 1, 1))
                    if exists(late - 1):
                        dve.wait_ge(squared, nth(late - 1, EXP_SQUARINGS, 1))
                    nc.vector.scalar_tensor_tensor(out=powers[:, 0], in0=exp_tanh[:], scalar=1.0, in1=exp_rec[:],
                                                   op0=ALU.add, op1=ALU.mult).then_inc(root_done, 1)
                if s == 7:
                    dve.wait_ge(squared, nth(late, EXP_SQUARINGS, EXP_SQUARINGS))
                    dve.wait_ge(chosen_done, nth(late, 1, 1))
                    nc.vector.tensor_reduce(exp_sum[:], powers[:, EXP_SQUARINGS], AX_X, ALU.add)\
                        .then_inc(exp_sum_done, 1)
                    nc.vector.tensor_tensor(exp_chosen[:], powers[:, EXP_SQUARINGS], chosen[:], ALU.mult)\
                        .then_inc(exp_chosen_done, 1)
                    dve.wait_ge(exp_sum_done, nth(late, 1, 1))
                    nc.vector.reciprocal(exp_sum_rec[:], exp_sum[:]).then_inc(exp_sum_rec_done, 1)
                    dve.wait_ge(exp_sum_rec_done, nth(late, 1, 1))
                    dve.wait_ge(exp_chosen_done, nth(late, 1, 1))
                    if exists(late - 1):
                        dve.wait_ge(comb_turned, nth(late - 1, 1, 1))
                    nc.vector.tensor_tensor(comb_tm[:].rearrange("p e t -> p t e"), exp_chosen[:],
                                            exp_sum_rec[:].rearrange("p (t o) -> p t o", o=1)
                                            .broadcast_to([P, TILES, E]), ALU.mult).then_inc(comb_done, 1)

            def slot(s, experts, late, early):
                if s == (4 if late and first_of_all(late) else 5) and late:
                    dve.wait_ge(h2_hi_done, nth(late, 1, 1))
                    nc.vector.tensor_tensor(h2_lo[:, late.slot, :], ps2[:], h2_hi[:, late.slot, :].bitcast(F32),
                                            ALU.subtract).then_inc(h2_lo_done, 1)
                if experts:
                    if s:
                        scale_expert(experts, s - 1)
                    elif exists(experts - 1):
                        scale_expert(experts - 1, E - 1)
                if early and s == 3 and has_next(early):
                    first_stats(early + 1)
                if late:
                    late_work(s, late)
                if early:
                    early_work(s, early)
                if s == 7 and experts and exists(experts - 1):
                    add_residual(experts - 1)
                if experts and s + 1 in SPLIT:
                    gelu_low(experts, s + 1)
                if late and s == 7 and 0 in SPLIT:
                    gelu_low(late, 0)

            run(dve, slot)
            scale_expert(Group(BATCHES - 1, 1), E - 1)
            add_residual(Group(BATCHES - 1, 1))

        @block.tensor
        def _(pe):
            pe.wait_ge(s_weights["wmod"], 16)
            pe.wait_ge(silu_done, 1)
            for n in range(6):
                bank = ps0 if n < 2 else ps2
                ins = nc.tensor.matmul(bank[:, n * BATCHES:(n + 1) * BATCHES], wmod_sb[:, n * P:(n + 1) * P],
                                       silu_c[:], start=True, stop=True)
                if n in (1, 5):
                    ins.then_inc(mods_ps_done, 1)

            def product(dst, w_hi, w_lo, x_hi, x_lo):
                nc.tensor.matmul(dst, w_hi, x_hi, start=True, stop=False)
                nc.tensor.matmul(dst, w_lo, x_hi, start=False, stop=False)
                return nc.tensor.matmul(dst, w_hi, x_lo, start=False, stop=True)

            def turn_tiles(dst, src):
                for t in range(TILES):
                    ins = nc.tensor.transpose(dst[:, tile(t)], src[:, tile(t)], ident[:])
                return ins

            def project(dst, which, x_hi, x_lo):
                return product(dst, attn_hi[:, which, :], attn_lo[:, which, :], x_hi[:], x_lo[:])

            def up(g, e, chunks=(0, 1)):
                if e == 0:
                    pe.wait_ge(h2_hi_done, nth(g, 1, 1))
                    pe.wait_ge(h2_lo_done, nth(g, 1, 1))
                for f in chunks:
                    c = 2 * e + f
                    before, back = chunk_before(c)
                    if exists(g - back):
                        pe.wait_ge(gelu_done, nth(g - back, CHUNKS, before + 1))
                    w = slice(c * P, (c + 1) * P)
                    product(up_ps[:, UP_BANK[c], :], w1_hi[:, w], w1_lo[:, w],
                            h2_hi[:, g.slot, :], h2_lo[:, g.slot, :]).then_inc(up_done, 1)

            def down(g, e):
                if e >= 2:
                    pe.wait_ge(scaled_done, nth(g, E, e - 1))
                elif exists(g - 1):
                    pe.wait_ge(scaled_done, nth(g - 1, E, e + 7))
                dst = down_ps[:, e % 2, :]
                if e in SPLIT:
                    for f in range(2):
                        pe.wait_ge(gelu_hi_done, nth(g, 2 * NS, 2 * split_before[e] + f + 1))
                        nc.tensor.matmul(dst, w2_hi[:, e, f, :], gelu_hi[:, e % 2, f, :], start=f == 0, stop=False)
                        nc.tensor.matmul(dst, w2_lo[:, e, f, :], gelu_hi[:, e % 2, f, :], start=False, stop=False)
                    pe.wait_ge(gelu_lo_done, nth(g, NS, split_before[e] + 1))
                    for f in range(2):
                        ins = nc.tensor.matmul(dst, w2_hi[:, e, f, :], gelu_lo[:, e % 2, f, :], start=False,
                                               stop=f == 1)
                else:
                    for f in range(2):
                        pe.wait_ge(gelu_done, nth(g, CHUNKS, 2 * e + f + 1))
                        ins = nc.tensor.matmul(dst, w2[:, e, f, :], gelu_cm[:, e % 2, f, :], start=f == 0, stop=f == 1)
                ins.then_inc(down_done, 1)

            def turn_gated(g):
                pe.wait_ge(gated_done, nth(g, 1, 1))
                turn_tiles(ps0, gated_cm).then_inc(gated_turned, 1)

            def make_rows(b):
                if b == 0:
                    pe.wait_ge(row_cols_done, 1)
                if b >= 2:
                    pe.wait_ge(rows_done, b - 1)
                for j in range(4):
                    ins = nc.tensor.matmul(row_bank(b)[:, j * P:(j + 1) * P],
                                           row_cols[:, b, j:j + 1].broadcast_to([P, P]), ident[:],
                                           start=True, stop=True)
                ins.then_inc(rows_ps_done, 1)

            def slot(s, experts, late, early):
                if late and first_of_all(late) and s < BATCHES - 1:
                    make_rows(s + 1)
                if experts and s < 7:
                    up(experts, s + 1, (0,))
                if s == 5 and late:
                    pe.wait_ge(h2_done, nth(late, 1, 1))
                    if exists(late - 1):
                        pe.wait_ge(comb_em_done, nth(late - 1, 1, 1))
                    else:
                        pe.wait_ge(gate_split, 1)
                    turn_tiles(ps2, h2_tm).then_inc(h2_turned, 1)
                if s == 0 and experts:
                    pe.wait_ge(comb_done, nth(experts, 1, 1))
                    nc.tensor.transpose(ps2[0:E * TILES, 0:P], comb_tm[:].rearrange("p e t -> p (e t)"), ident[:])\
                        .then_inc(comb_turned, 1)
                if experts and s < 7:
                    up(experts, s + 1, (1,))
                if s == 6 and late:
                    if not exists(late - 1):
                        pe.wait_ge(gate_split, 1)
                    pe.wait_ge(h2_lo_done, nth(late, 1, 1))
                    for t in range(TILES):
                        both = ps2[:, 2 * t * E:2 * (t + 1) * E]
                        nc.tensor.matmul(both, h2_hi[:, late.slot, tile(t)],
                                         gate_split_w[:].rearrange("p w e -> p (w e)"), start=True, stop=False)
                        ins = nc.tensor.matmul(both[:, 0:E], h2_lo[:, late.slot, tile(t)], gate_split_w[:, 0, :],
                                               start=False, stop=True)
                    ins.then_inc(logits_ps_done, 1)
                if s == 7 and late:
                    if not exists(late - 1):
                        pe.wait_ge(w1_split, 1)
                    up(late, 0)
                if s == 0 and late:
                    pe.wait_ge(z_done, nth(late, 1, 1))
                    turn_tiles(ps1, z_cm).then_inc(z_turned, 1)
                if s == 0 and early:
                    pe.wait_ge(n1_done, nth(early, 1, 1))
                    if not exists(early - 1):
                        pe.wait_ge(consts, 5)
                        pe.wait_ge(mod_cols_done, 1)
                    if experts and exists(experts - 2):
                        pe.wait_ge(out_done, nth(experts - 2, 1, 1))
                    turn_tiles(ps0, n1_tm).then_inc(n1_turned, 1)
                if s == 6:
                    if experts and exists(experts - 1):
                        if early:
                            pe.wait_ge(o_done, nth(early, 1, 1))
                        turn_gated(experts - 1)
                    if early:
                        pe.wait_ge(o_hi_done, nth(early, 1, 1))
                        pe.wait_ge(o_lo_done, nth(early, 1, 1))
                        pe.wait_ge(kv_done, nth(early, 1, 1))
                        project(ps1[:], OUT, o_hi, o_lo).then_inc(out_ps_done, 1)
                if experts:
                    if s == 0 and not exists(experts - 1):
                        pe.wait_ge(w2_split, 1)
                        pe.wait_ge(rows_done, BATCHES)
                    down(experts, s)
                if s == 2 and early:
                    if not exists(early - 1):
                        pe.wait_ge(attn_split, 1)
                    pe.wait_ge(h_hi_done, nth(early, 1, 1))
                    pe.wait_ge(h_lo_done, nth(early, 1, 1))
                    project(ps0[:], V, h_hi, h_lo).then_inc(v_ps_done, 1)
                    if late:
                        pe.wait_ge(nz_done, nth(late, 1, 1))
                    project(ps1[:], BETA, h_hi, h_lo).then_inc(beta_ps_done, 1)
                if s == 3 and early:
                    pe.wait_ge(beta_tanh_done, nth(early, 1, 1))
                    project(ps1[:], K, h_hi, h_lo).then_inc(k_ps_done, 1)
                    pe.wait_ge(vsum_done, nth(early, 1, 1))
                    project(ps0[:], Q, h_hi, h_lo).then_inc(q_ps_done, 1)
                    if first_of_all(early):
                        make_rows(0)
                        pe.wait_ge(gate_gamma_done, 1)
                        nc.tensor.matmul(ps2[:, 0:E], mean_w[:], gate_gamma[:], start=True, stop=True)
                        nc.tensor.matmul(ps2[:, E:2 * E], cols[:, 3:4].broadcast_to([P, P]), gate[:],
                                         start=True, stop=True).then_inc(gate_ps_done, 1)

            run(pe, slot)
            turn_gated(Group(BATCHES - 1, 1))

def kernel(**inputs):
    import numpy as np
    import concourse.bacc as bacc
    from concourse import mybir as mb
    from concourse.bass_utils import run_bass_kernel_spmd

    def a(name):
        return np.asarray(inputs["L0_" + name])

    x = a("attn_x")
    B, S, C = x.shape
    groups = B * S // TOK
    E, F, _ = a("ffn_w1").shape
    arrays = {
        "x": x.reshape(groups, TILES, P, C).transpose(0, 2, 1, 3).reshape(groups, P, TOK),
        "cT": a("c").T,
        "wmod": a("wmod"),
        "wq": a("attn_Wq"), "wk": a("attn_Wk"), "wv": a("attn_Wv"), "wbeta": a("attn_Wbeta"),
        "b_beta": a("attn_b_beta"), "wo": a("attn_Wo"),
        "vectors": np.stack([a("attn_b_o"), a("ffn_ln_gamma"), a("ffn_ln_beta"), a("attn_ln_g"), a("attn_ln_b")], 1),
        "gateT": a("ffn_gate_w").T,
        "w1T": a("ffn_w1").transpose(2, 0, 1).reshape(C, E * F),
        "w2T": a("ffn_w2").reshape(E, C, F // P, P).transpose(3, 0, 2, 1),
    }
    arrays = {n: np.ascontiguousarray(v) for n, v in arrays.items()}
    nc = bacc.Bacc("TRN2", target_bir_lowering=False, num_devices=1)
    args = [nc.dram_tensor("in_" + n, v.shape, mb.dt.from_np(v.dtype), kind="ExternalInput").ap()
            for n, v in arrays.items()]
    out = nc.dram_tensor("out", (groups, P, TOK), mb.dt.float32, kind="ExternalOutput").ap()
    adaln_moe_kernel(nc, *args, out)
    r = run_bass_kernel_spmd(nc, [{"in_" + n: v for n, v in arrays.items()}], core_ids=[0])
    got = r.results[0]["out"]
    return got.reshape(groups, P, TILES, C).transpose(0, 2, 1, 3).reshape(B, S, C)
```
